# Optimizing a Trainium2 kernel written in Bass

```python
import numpy as np
import jax
import jax.numpy as jnp

def _softmax(x, axis=-1):
    return jax.nn.softmax(x, axis=axis)

def _gelu(x):
    return jax.nn.gelu(x, approximate=True)

def _silu(x):
    return jax.nn.silu(x)

def _sigmoid(x):
    return jax.nn.sigmoid(x)

def _layernorm(x, axis=-1, eps=1e-05):
    m = jnp.mean(x, axis=axis, keepdims=True)
    v = jnp.var(x, axis=axis, keepdims=True)
    return (x - m) / jnp.sqrt(v + eps)

def _scatter_add(tgt, idx, src, axis=0):
    return tgt.at[idx].add(src)

def _segment_sum(src, seg, n):
    return jax.ops.segment_sum(src, seg, n)
kernel_name = 'mk_gnn_preln_d4_gnn_r8_4be431'

def setup_inputs(seed: int=0):
    np.random.seed(seed)
    _w = jnp.asarray

    def _rec_inputs():
        import jax
        import jax.numpy as jnp
        _gk = jax.random.key(seed)
        x = -0.000202 + 1 * jax.random.normal(jax.random.fold_in(_gk, 1), (6250, 128), jnp.float32)
        _s = jax.random.randint(jax.random.fold_in(_gk, 2), (50000,), 0, 6250, jnp.int32)
        _d = jax.random.randint(jax.random.fold_in(_gk, 3), (50000,), 0, 6250, jnp.int32)
        _loop = jnp.arange(6250, dtype=jnp.int32)
        src = jnp.concatenate([_s, _d, _loop])
        dst = jnp.concatenate([_d, _s, _loop])
        _o = jnp.argsort(dst, stable=True)
        src = src[_o]
        dst = dst[_o]
        edge_attr_128 = -5.16925e-05 + 1.00005 * jax.random.normal(jax.random.fold_in(_gk, 11), (106250, 128), jnp.float32)
        return (x, src, dst, edge_attr_128)
    x, src, dst, edge_attr_128 = _rec_inputs()

    def _L0_gnn_setup():
        import jax, jax.numpy as jnp
        import numpy as np
        N_NODES = 6250
        N_EDGES = 100000
        D_IN = 128
        D_OUT = 128
        key = jax.random.key(seed)
        ks = jax.random.split(key, 8)
        x = jax.random.normal(ks[0], (N_NODES, D_IN), dtype=jnp.float32)
        edge_index = jax.random.randint(ks[1], (2, N_EDGES), 0, N_NODES, dtype=jnp.int64)
        edge_attr = jax.random.normal(ks[2], (N_EDGES, D_IN), dtype=jnp.float32)
        s1 = 1.0 / np.sqrt(D_IN)
        s2 = 1.0 / np.sqrt(D_OUT)
        W1 = jax.random.uniform(ks[3], (D_IN, D_OUT), jnp.float32, -s1, s1)
        b1 = jax.random.uniform(ks[4], (D_OUT,), jnp.float32, -s1, s1)
        W2 = jax.random.uniform(ks[5], (D_OUT, D_OUT), jnp.float32, -s2, s2)
        b2 = jax.random.uniform(ks[6], (D_OUT,), jnp.float32, -s2, s2)
        eps = jnp.zeros((), dtype=jnp.float32)
        return {'x': x, 'edge_index': edge_index, 'edge_attr': edge_attr, 'W1': W1, 'b1': b1, 'W2': W2, 'b2': b2, 'eps': eps}
    _L0_gnn_all = _L0_gnn_setup()
    _L0_gnn_in = {k: v for k, v in _L0_gnn_all.items() if k in ('W1', 'b1', 'W2', 'b2', 'eps')}
    del _L0_gnn_all

    def _L1_gnn_setup():
        import jax, jax.numpy as jnp
        import numpy as np
        N_NODES = 6250
        N_EDGES = 100000
        D_IN = 128
        D_HID = 128
        BN_EPS = 1e-05
        key = jax.random.key(seed)
        ks = jax.random.split(key, 8)
        x = jax.random.normal(ks[0], (N_NODES, D_IN), dtype=jnp.float32)
        edge_index = jax.random.randint(ks[1], (2, N_EDGES), 0, N_NODES, dtype=jnp.int32)
        W1 = jax.random.normal(ks[2], (D_IN, D_HID), dtype=jnp.float32) * (1.0 / np.sqrt(D_IN))
        b1 = jnp.zeros((D_HID,), dtype=jnp.float32)
        W2 = jax.random.normal(ks[3], (D_HID, D_IN), dtype=jnp.float32) * (1.0 / np.sqrt(D_HID))
        b2 = jnp.zeros((D_IN,), dtype=jnp.float32)
        gamma = jnp.ones((D_IN,), dtype=jnp.float32)
        beta = jnp.zeros((D_IN,), dtype=jnp.float32)
        return {'x': x, 'edge_index': edge_index, 'W1': W1, 'b1': b1, 'W2': W2, 'b2': b2, 'gamma': gamma, 'beta': beta}
    _L1_gnn_all = _L1_gnn_setup()
    _L1_gnn_in = {k: v for k, v in _L1_gnn_all.items() if k in ('W1', 'b1', 'W2', 'b2', 'gamma', 'beta')}
    del _L1_gnn_all

    def _L2_gnn_setup():
        import jax, jax.numpy as jnp
        import numpy as np
        N_NODES = 12500
        N_EDGES = 200000
        IN_F = 128
        HEADS = 4
        OUT_F = 32
        NEG_SLOPE = 0.2

        def _xavier(key, shape):
            fan_in, fan_out = (shape[0], shape[-1])
            if len(shape) == 3:
                fan_in, fan_out = (1, shape[1] * shape[2])
            limit = float(np.sqrt(6.0 / (fan_in + fan_out)))
            return jax.random.uniform(key, shape, jnp.float32, -limit, limit)
        key = jax.random.key(seed)
        k_feat, k_ei, k_wl, k_wr, k_att = jax.random.split(key, 5)
        features = jax.random.normal(k_feat, (N_NODES, IN_F), jnp.float32)
        edge_index = jax.random.randint(k_ei, (2, N_EDGES), 0, N_NODES, jnp.int64)
        weight_l = _xavier(k_wl, (IN_F, HEADS * OUT_F))
        weight_r = _xavier(k_wr, (IN_F, HEADS * OUT_F))
        att = _xavier(k_att, (1, HEADS, OUT_F))
        bias = jnp.zeros((HEADS * OUT_F,), jnp.float32)
        return {'features': features, 'edge_index': edge_index, 'weight_l': weight_l, 'weight_r': weight_r, 'att': att, 'bias': bias}
    _L2_gnn_all = _L2_gnn_setup()
    _L2_gnn_in = {k: v for k, v in _L2_gnn_all.items() if k in ('weight_l', 'weight_r', 'att', 'bias')}
    del _L2_gnn_all

    def _L3_gnn_setup():
        import jax, jax.numpy as jnp
        import numpy as np
        N, D, E = (12500, 128, 200000)

        def gcn_conv(x, edge_index, W, b):
            n = x.shape[0]
            loops = jnp.arange(n, dtype=edge_index.dtype)
            src = jnp.concatenate([edge_index[0], loops])
            dst = jnp.concatenate([edge_index[1], loops])
            h = x @ W
            ones = jnp.ones(src.shape[0], dtype=x.dtype)
            deg = jax.ops.segment_sum(ones, dst, num_segments=n)
            dinv = jax.lax.rsqrt(deg)
            norm = dinv[src] * dinv[dst]
            msgs = h[src] * norm[:, None]
            agg = jax.ops.segment_sum(msgs, dst, num_segments=n)
            return agg + b
        key = jax.random.key(seed)
        k1, k2, k3, k4, k5 = jax.random.split(key, 5)
        x = jax.random.normal(k1, (N, D), dtype=jnp.float32)
        edge_index = jax.random.randint(k2, (2, E), 0, N, dtype=jnp.int64)
        bound = float(np.sqrt(6.0 / (D + D)))
        W_gcn = jax.random.uniform(k3, (D, D), jnp.float32, -bound, bound)
        b_gcn = jnp.zeros((D,), jnp.float32)
        lb = float(1.0 / np.sqrt(D))
        W_ln = jax.random.uniform(k4, (D, D), jnp.float32, -lb, lb)
        return {'x': x, 'edge_index': edge_index, 'W_gcn': W_gcn, 'b_gcn': b_gcn, 'W_ln': W_ln}
    _L3_gnn_all = _L3_gnn_setup()
    _L3_gnn_in = {k: v for k, v in _L3_gnn_all.items() if k in ('W_gcn', 'b_gcn', 'W_ln')}
    del _L3_gnn_all
    return {'x': x, 'src': src, 'dst': dst, 'edge_attr_128': edge_attr_128, 'L0_gnn_W1': _L0_gnn_in['W1'], 'L0_gnn_b1': _L0_gnn_in['b1'], 'L0_gnn_W2': _L0_gnn_in['W2'], 'L0_gnn_b2': _L0_gnn_in['b2'], 'L0_gnn_eps': _L0_gnn_in['eps'], 'L1_gnn_W1': _L1_gnn_in['W1'], 'L1_gnn_b1': _L1_gnn_in['b1'], 'L1_gnn_W2': _L1_gnn_in['W2'], 'L1_gnn_b2': _L1_gnn_in['b2'], 'L1_gnn_gamma': _L1_gnn_in['gamma'], 'L1_gnn_beta': _L1_gnn_in['beta'], 'L2_gnn_weight_l': _L2_gnn_in['weight_l'], 'L2_gnn_weight_r': _L2_gnn_in['weight_r'], 'L2_gnn_att': _L2_gnn_in['att'], 'L2_gnn_bias': _L2_gnn_in['bias'], 'L3_gnn_W_gcn': _L3_gnn_in['W_gcn'], 'L3_gnn_b_gcn': _L3_gnn_in['b_gcn'], 'L3_gnn_W_ln': _L3_gnn_in['W_ln']}

def reference(x, src, dst, edge_attr_128, L0_gnn_W1, L0_gnn_b1, L0_gnn_W2, L0_gnn_b2, L0_gnn_eps, L1_gnn_W1, L1_gnn_b1, L1_gnn_W2, L1_gnn_b2, L1_gnn_gamma, L1_gnn_beta, L2_gnn_weight_l, L2_gnn_weight_r, L2_gnn_att, L2_gnn_bias, L3_gnn_W_gcn, L3_gnn_b_gcn, L3_gnn_W_ln):
    import jax
    import jax.numpy as jnp

    def _L0_gnn_ref(x, edge_index, edge_attr, W1, b1, W2, b2, eps):
        import jax, jax.numpy as jnp
        import numpy as np
        N_NODES = 6250
        N_EDGES = 100000
        D_IN = 128
        D_OUT = 128
        src = edge_index[0]
        dst = edge_index[1]
        msg = jax.nn.relu(x[src] + edge_attr)
        agg = jax.ops.segment_sum(msg, dst, num_segments=N_NODES)
        h = (1.0 + eps) * x + agg
        h = jax.nn.relu(h @ W1 + b1)
        out = h @ W2 + b2
        return out

    def _L1_gnn_ref(x, edge_index, W1, b1, W2, b2, gamma, beta):
        import jax, jax.numpy as jnp
        import numpy as np
        N_NODES = 6250
        N_EDGES = 100000
        D_IN = 128
        D_HID = 128
        BN_EPS = 1e-05
        n = x.shape[0]
        src, dst = (edge_index[0], edge_index[1])
        aggr = jax.ops.segment_sum(x[src], dst, num_segments=n)
        h = x + aggr
        h = jax.nn.relu(h @ W1 + b1) @ W2 + b2
        mean = jnp.mean(h, axis=0)
        var = jnp.var(h, axis=0)
        h = (h - mean) * jax.lax.rsqrt(var + BN_EPS) * gamma + beta
        return h + x

    def _L2_gnn_ref(features, edge_index, weight_l, weight_r, att, bias):
        import jax, jax.numpy as jnp
        import numpy as np
        N_NODES = 12500
        N_EDGES = 200000
        IN_F = 128
        HEADS = 4
        OUT_F = 32
        NEG_SLOPE = 0.2

        def _xavier(key, shape):
            fan_in, fan_out = (shape[0], shape[-1])
            if len(shape) == 3:
                fan_in, fan_out = (1, shape[1] * shape[2])
            limit = float(np.sqrt(6.0 / (fan_in + fan_out)))
            return jax.random.uniform(key, shape, jnp.float32, -limit, limit)
        num_nodes = features.shape[0]
        src, tgt = (edge_index[0], edge_index[1])
        h_l = (features @ weight_l).reshape(num_nodes, HEADS, OUT_F)
        h_r = (features @ weight_r).reshape(num_nodes, HEADS, OUT_F)
        x_i = h_l[tgt]
        x_j = h_r[src]
        e = jnp.sum(jax.nn.leaky_relu(x_i + x_j, NEG_SLOPE) * att, axis=-1)
        seg_max = jax.ops.segment_max(e, tgt, num_segments=num_nodes)
        exp_e = jnp.exp(e - seg_max[tgt])
        seg_sum = jax.ops.segment_sum(exp_e, tgt, num_segments=num_nodes)
        alpha = exp_e / jnp.clip(seg_sum[tgt], 1e-16)
        messages = x_j * alpha[..., None]
        out = jax.ops.segment_sum(messages, tgt, num_segments=num_nodes)
        out = out.reshape(num_nodes, HEADS * OUT_F) + bias
        return out

    def _L3_gnn_ref(x, edge_index, W_gcn, b_gcn, W_ln):
        import jax, jax.numpy as jnp
        import numpy as np
        N, D, E = (12500, 128, 200000)

        def gcn_conv(x, edge_index, W, b):
            n = x.shape[0]
            loops = jnp.arange(n, dtype=edge_index.dtype)
            src = jnp.concatenate([edge_index[0], loops])
            dst = jnp.concatenate([edge_index[1], loops])
            h = x @ W
            ones = jnp.ones(src.shape[0], dtype=x.dtype)
            deg = jax.ops.segment_sum(ones, dst, num_segments=n)
            dinv = jax.lax.rsqrt(deg)
            norm = dinv[src] * dinv[dst]
            msgs = h[src] * norm[:, None]
            agg = jax.ops.segment_sum(msgs, dst, num_segments=n)
            return agg + b
        out = gcn_conv(x, edge_index, W_gcn, b_gcn)
        out = jax.nn.relu(out)
        out = out @ W_ln.T
        out = out + x
        return jax.nn.relu(out)
    edge_index = jnp.stack([src, dst])
    h = jnp.maximum(_layernorm(x, axis=-1), 0.0)
    x = x + _L0_gnn_ref(h, edge_index, edge_attr_128, L0_gnn_W1, L0_gnn_b1, L0_gnn_W2, L0_gnn_b2, L0_gnn_eps)
    h = jnp.maximum(_layernorm(x, axis=-1), 0.0)
    x = x + _L1_gnn_ref(h, edge_index, L1_gnn_W1, L1_gnn_b1, L1_gnn_W2, L1_gnn_b2, L1_gnn_gamma, L1_gnn_beta)
    h = jnp.maximum(_layernorm(x, axis=-1), 0.0)
    x = x + _L2_gnn_ref(h, edge_index, L2_gnn_weight_l, L2_gnn_weight_r, L2_gnn_att, L2_gnn_bias)
    h = jnp.maximum(_layernorm(x, axis=-1), 0.0)
    x = x + _L3_gnn_ref(h, edge_index, L3_gnn_W_gcn, L3_gnn_b_gcn, L3_gnn_W_ln)
    return x

_drawn_inputs = setup_inputs


def setup_inputs(seed=0):
    import zlib

    import numpy as np

    out = dict(_drawn_inputs(seed))
    spreads = {'L1_gnn_b1': (0.0, 2.0),
     'L1_gnn_b2': (0.0, 2.0),
     'L1_gnn_gamma': (1.0, 0.2),
     'L1_gnn_beta': (0.0, 0.278),
     'L2_gnn_bias': (0.0, 0.315),
     'L3_gnn_b_gcn': (0.0, 0.8)}
    factors = {'L0_gnn_b1': 8.0, 'L0_gnn_b2': 3.1, 'L2_gnn_weight_l': 23.616, 'L2_gnn_att': 8.0}
    for name, (base, spread) in spreads.items():
        noise = np.random.default_rng([zlib.crc32(name.encode()), seed]).standard_normal(out[name].shape)
        drawn = base * np.exp(spread * noise) if base else spread * noise
        out[name] = jnp.asarray(drawn.astype(out[name].dtype))
    for name, factor in factors.items():
        out[name] = (out[name] * factor).astype(out[name].dtype)
    return out
```

```python
from contextlib import ExitStack

import concourse.bass as bass
from concourse import mybir

f32 = mybir.dt.float32
i32 = mybir.dt.int32
ALU = mybir.AluOpType
ACT = mybir.ActivationFunctionType
AX = mybir.AxisListType

P = 128
BIG = 1e30
LN_EPS = 1e-5
BN_EPS = 1e-5
SLOPE = 0.2
HEADS = 4
HF = P // HEADS

GT = 4
RING = 4
CB = 4


class Chain:

    def __init__(self, eng, sem):
        self.eng, self.sem, self.base, self.n = eng, sem, 0, 0

    def at(self, step, per):
        self.n, self.left = step * per + self.base, per

    def done(self, steps, per):
        self.base += steps * per
        self.n = self.base

    def link(self, ins):
        ins.then_inc(self.sem, 1)
        self.n = self.n + 1
        self.eng.wait_ge(self.sem, self.n)

    def one(self, ins):
        self.base += 1
        self.n = self.base
        ins.then_inc(self.sem, 1)
        self.eng.wait_ge(self.sem, self.n)


def build(nc, x, src, dst, edge_attr, g0_w1, g0_b1, g0_w2, g0_b2, g0_eps, g1_w1, g1_b1, g1_w2, g1_b2,
          g1_gamma, g1_beta, g2_wl, g2_wr, g2_att, g2_bias, g3_w, g3_b, g3_wln, out):
    N = x.shape[0]
    E = src.shape[0]
    ITERS = -(-E // (P * GT * RING))
    GROUPS = ITERS * RING
    T = GROUPS * GT
    NB = -(-N // P)
    CHUNKS = -(-(NB + 1) // CB)
    NBP = CHUNKS * CB
    NW = NBP * P
    CHAINS = 32
    SEG = T // CHAINS
    SL = SEG * P
    assert SEG * CHAINS == T and HEADS * CHAINS == P and N + P <= NW and CHUNKS % 2 == 1
    FULL = E // P
    TG = -(-T // P)
    REST = N - (NB - 1) * P

    ctx = ExitStack()
    with ctx:
        def sb(name, shape, dt=f32):
            return ctx.enter_context(nc.sbuf_tensor(name, shape, dt))

        def sem(name):
            return ctx.enter_context(nc.semaphore(name))

        def dram(name, shape, dt=f32):
            return nc.dram_tensor(name, shape, dt, kind="Internal").ap()

        table = [dram(f"table{n}", [NW, P]) for n in range(4)]
        hl_table = dram("hl_table", [NW, P])
        xj_store = dram("xj_store", [GROUPS, P, GT * P])
        dst_line = dram("dst_line", [T * P + 2], i32)

        X = sb("X", [P, NBP, P])
        H = sb("H", [P, NBP, P])
        HT = sb("HT", [P, NW + 4])
        AD = sb("AD", [P, 2, NW + 4])
        ACC, DEG = AD[:, 0, :], AD[:, 1, :]
        SRC = sb("SRC", [P, T])
        LD = sb("LD", [P, T])
        WIN = sb("WIN", [1, T], i32)
        EA = sb("EA", [P, RING * GT, P])
        G = sb("G", [P, RING * GT, P])
        MSG = sb("MSG", [P, 2 * GT, P])
        OH = sb("OH", [P, 2 * GT, P])
        OHT = sb("OHT", [P, 2 * GT, P])
        EL = sb("EL", [P, T, HEADS])
        IDX = sb("IDX", [P, RING * GT], i32)
        ident = sb("ident", [P, P])
        iota_row = sb("iota_row", [P, P])
        ones = sb("ones", [P, P])
        W = {n: sb("w_" + n, [P, P]) for n in ("g0_1", "g0_2", "g1_1", "g1_2", "g3", "ln_raw", "ln")}
        WLR = sb("w_lr", [P, 2 * P])
        att4 = sb("att4", [P, HEADS])
        cols = sb("cols", [P, 8])
        rows = sb("rows", [1, 2, P])
        ST = sb("ST", [P, max(2 * CB, CHUNKS), 6])
        MV = sb("MV", [P, 2 * CB, 2])
        MEAN, VAR, SD, RS, NM = (sb(n, [P, NBP]) for n in ("MEAN", "VAR", "SD", "RS", "NM"))
        consts = sb("consts", [P, 2])
        small = sb("small", [P, 8])
        carry_rows = sb("carry_rows", [1, 2 * P])
        carry = sb("carry", [1, HEADS, CHAINS + 1])
        ends = sb("ends", [1, 2], i32)
        PS = ctx.enter_context(nc.psum_tensor("PS", [P, 8, GT * P], f32))

        S, F = HT[:, 0:SL], HT[:, SL:2 * SL]
        NEW = ACC[:, 0:SL + 1]
        KEEP = ACC[:, SL + 1:2 * SL + 2]
        assert 2 * SL + 2 <= NW + 4
        raw = G[:].bitcast(i32)
        assert TG * 2 <= RING * GT
        dst_raw, src_raw = raw[:, 0:TG, :], raw[:, TG:2 * TG, :]
        dst_f, src_f = EA[:, 0:TG, :], EA[:, TG:2 * TG, :]
        loc_f = MSG[:, 0:TG, :]
        B01, B02, B11, B3, GAM, BET, E1, ATT = range(8)

        s_pre = sem("constants_ready")
        s_w = sem("weights_loaded")
        s_x = sem("x_loaded")
        s_raw = sem("edges_loaded")
        s_f = sem("edges_as_float")
        s_tp0 = sem("edges_transposed")
        s_ix = sem("edge_tables_ready")
        s_line = sem("dst_line_written")
        s_chain = sem("vector_step_done")
        s_achain = sem("scalar_step_done")
        s_x1 = sem("rows_updated")
        s_var = sem("variances_ready")
        s_sd = sem("deviations_ready")
        s_bsd = sem("batch_deviation_ready")
        s_bva = sem("batch_variance_ready")
        s_dsd = sem("degree_roots_ready")
        s_ln = sem("norm_scales_ready")
        s_h = sem("h_ready")
        s_tab = sem("table_written")
        s_tp = sem("h_transposed")
        s_acc0 = sem("accumulator_started")
        s_ht = sem("ht_ready")
        s_gath = [sem(f"gathered_{q}") for q in range(RING)]
        s_ea = [sem(f"edge_rows_loaded_{q}") for q in range(RING)]
        s_xj = [sem(f"xj_stored_{q}") for q in range(RING)]
        s_settle = sem("settled")
        s_idx = sem("indices_ready")
        s_msg = sem("messages_ready")
        s_relu = sem("messages_rectified")
        s_oh = sem("onehots_ready")
        s_mm = sem("group_products_done")
        s_add = sem("tile_added")
        s_m1 = sem("mlp_in_product")
        s_z = sem("mlp_hidden_ready")
        s_m2 = sem("row_product_done")
        s_yp = sem("layer1_output_product")
        s_y = sem("layer1_output_ready")
        s_dv = sem("sums_times_dinv")
        s_bn = sem("batch_norm_done")
        s_bns = sem("batch_norm_scales_ready")
        s_ohtp = sem("onehots_transposed")
        s_oht = sem("transposed_onehots_copied")
        s_zz = sem("edge_sums_ready")
        s_sl = sem("sloped_sums_ready")
        s_lk = sem("leaky_ready")
        s_lg = sem("logit_product_done")
        s_el = sem("logits_copied")
        s_lrp = sem("table_product_done")
        s_lrc = sem("table_rows_staged")
        s_lrt = [sem(f"staged_rows_written_{par}") for par in range(2)]
        s_sort = sem("logits_by_chain")
        s_sc = sem("scan_input_transposed")
        s_scc = sem("scan_input_copied")
        s_seg = sem("scan_lines_loaded")
        s_cr = sem("chain_ends_ready")
        s_crt = sem("chain_ends_transposed")
        s_ci = sem("carries_ready")
        s_cit = sem("carries_transposed")
        s_sub = sem("logits_shifted")
        s_exp = sem("exponentials_ready")
        s_al = sem("weights_ready")
        s_alt = sem("weights_transposed")
        s_alc = sem("weights_copied")
        s_az = sem("accumulator_cleared")
        s_out = sem("output_written")

        CREDIT = 4
        mm = lambda g: g + (CREDIT + 1)
        added = lambda g: g * GT + (GT * (CREDIT + 1))

        lr_stored = lambda par: 32 * (CHUNKS // 2 + 1 - par)
        g3_stored = lambda par: 48 * (CHUNKS // 2 + 1 - par)

        def settle(eng):
            eng.sem_inc(s_settle, 1)

        def window_starts(which, i):
            return nc.values_load_multi_w_load_instructions(
                WIN[0:1, bass.ds(i * (RING * GT), RING * GT)], engines=[which], min_val=0, max_val=N,
                skip_runtime_bounds_check_because="a window starts at a destination, or at N in the padding")[1]

        def chunks(eng, body):
            with eng.Fori(0, CHUNKS // 2) as j:
                body(2 * j, 0)
                body(2 * j + 1, 1)
            body(CHUNKS - 1, 0)

        def nodes(buf, c):
            return buf[:, bass.ds(c * CB, CB), :]

        def wide(buf, c):
            return buf[:, bass.ds(c * (CB * P), CB * P)]

        tail_slot = FULL - (ITERS - 1) * RING * GT

        def ea_before(q):
            return 16 * ITERS + (16 if q == tail_slot // GT else 0) + 16 * GT * ITERS

        A0, A1, AB, A3 = range(4)
        G0, G1, GA, G3 = range(4)

        block = ctx.enter_context(nc.Block())

        @block.sync
        def _(sp):
            def edges(view, ap, at):
                full = FULL // P
                last = FULL - full * P
                sp.dma_start(view[:, 0:full, :], ap[0:full * P * P].rearrange("(g p f) -> p g f", p=P, f=P)).then_inc(s_raw, 16)
                sp.dma_start(view[0:last, full, :], ap[full * P * P:FULL * P].rearrange("(p f) -> p f", f=P)).then_inc(s_raw, 16)
                sp.dma_start(view[last:last + 1, full, 0:E - FULL * P], ap[FULL * P:E].unsqueeze(0)).then_inc(s_raw, 16)

            sp.wait_ge(s_pre, 1)
            edges(dst_raw, dst, 0)
            edges(src_raw, src, 0)
            sp.dma_start(X[:, 0:NB - 1, :], x[0:(NB - 1) * P, :].rearrange("(b p) f -> p b f", p=P)).then_inc(s_x, 16)
            sp.dma_start(X[0:REST, NB - 1, :], x[(NB - 1) * P:N, :]).then_inc(s_x, 16)
            for name, ap in (("g0_1", g0_w1), ("g0_2", g0_w2), ("g1_1", g1_w1), ("g1_2", g1_w2), ("g3", g3_w), ("ln_raw", g3_wln)):
                sp.dma_start(W[name][:], ap).then_inc(s_w, 16)
            sp.dma_start(WLR[:, 0:P], g2_wl).then_inc(s_w, 16)
            sp.dma_start(WLR[:, P:2 * P], g2_wr).then_inc(s_w, 16)
            for c, ap in ((B01, g0_b1), (B02, g1_b2), (B11, g1_b1), (B3, g3_b), (GAM, g1_gamma), (BET, g1_beta)):
                sp.dma_start(cols[:, c:c + 1], ap.unsqueeze(1)).then_inc(s_w, 16)
            sp.dma_start(cols[:, ATT:ATT + 1], g2_att.rearrange("a h f -> (h f) a")).then_inc(s_w, 16)
            sp.dma_start(cols[:, E1:E1 + 1], g0_eps.unsqueeze(0).to_broadcast([P, 1])).then_inc(s_w, 16)
            for c, ap in ((0, g0_b2), (1, g2_bias)):
                sp.dma_start(rows[:, c, :], ap.unsqueeze(0)).then_inc(s_w, 16)
            sp.wait_ge(s_raw, 16 * 6)
            body = dst_line[1:T * P + 1]
            whole = T // P
            sp.dma_start(body[0:whole * P * P].rearrange("(g p f) -> p g f", p=P, f=P), dst_raw[:, 0:whole, :]).then_inc(s_line, 16)
            sp.dma_start(body[whole * P * P:T * P].rearrange("(p f) -> p f", f=P), dst_raw[0:T - whole * P, whole, :]).then_inc(s_line, 16)
            sp.dma_start(dst_line[0:1].unsqueeze(0), ends[:, 0:1]).then_inc(s_line, 16)
            sp.dma_start(dst_line[T * P + 1:T * P + 2].unsqueeze(0), ends[:, 1:2]).then_inc(s_line, 16)

            def store_table(n, count):
                view = table[n].rearrange("(b p) f -> p b f", p=P)

                def one(c, _):
                    sp.wait_ge(s_h, c + (CHUNKS * count + 1))
                    sp.dma_start(view[:, bass.ds(c * CB, CB), :], nodes(H, c)).then_inc(s_tab, 16)
                chunks(sp, one)

            store_table(0, 0)

            ea_view = edge_attr[0:FULL * P, :].rearrange("(t p) f -> p t f", p=P)

            def load_ea(i, q, tiles=GT):
                sp.wait_ge(s_msg, i * RING + (q + 1))
                sp.dma_start(EA[:, q * GT:q * GT + tiles, :], ea_view[:, bass.ds(i * (RING * GT) + q * GT, tiles), :]).then_inc(s_ea[q], 16)
            with sp.Fori(0, ITERS - 1) as i:
                for q in range(RING):
                    load_ea(i, q)
            for q in range(RING):
                here = min(GT, FULL - ((ITERS - 1) * RING + q) * GT)
                assert here > 0
                load_ea(ITERS - 1, q, here)
            sp.dma_start(EA[0:E - FULL * P, tail_slot, :], edge_attr[FULL * P:E, :]).then_inc(s_ea[tail_slot // GT], 16)

            store_table(1, 1)

            hl_view = hl_table.rearrange("(b p) f -> p b f", p=P)
            hr_view = table[2].rearrange("(b p) f -> p b f", p=P)

            def store_lr(c, par):
                sp.wait_ge(s_lrc, c + 1)
                sp.dma_start(hl_view[:, bass.ds(c * CB, CB), :], EA[:, par * CB:(par + 1) * CB, :]).then_inc(s_lrt[par], 16)
                sp.dma_start(hr_view[:, bass.ds(c * CB, CB), :], G[:, par * CB:(par + 1) * CB, :]).then_inc(s_lrt[par], 16)
            chunks(sp, store_lr)
            for par in range(2):
                sp.wait_ge(s_lrt[par], lr_stored(par))

            def load_windows(starts, q):
                for k in range(GT):
                    sp.dma_start(EA[:, q * GT + k, :], hl_table[bass.ds(starts[q * GT + k], P), :]).then_inc(s_ea[q], 16)

            def keep_xj(i, q):
                sp.wait_ge(s_gath[q], i * (16 * GT) + 16 * GT * (GA * ITERS + 1))
                sp.dma_start(xj_store[bass.ds(i * RING + q, 1), :, :].rearrange("a p f -> p (a f)"),
                             G[:, q * GT:(q + 1) * GT, :].rearrange("p k f -> p (k f)")).then_inc(s_xj[q], 16)
            starts = window_starts(mybir.EngineType.SP, 0)
            for q in range(RING):
                load_windows(starts, q)
            with sp.Fori(0, ITERS - 1) as i:
                starts = window_starts(mybir.EngineType.SP, i + 1)
                for q in range(RING):
                    keep_xj(i, q)
                    sp.wait_ge(s_zz, i * RING + (q + 1))
                    load_windows(starts, q)
            for q in range(RING):
                keep_xj(ITERS - 1, q)

            sp.wait_ge(s_line, 16 * 4)
            sp.wait_ge(s_zz, GROUPS)
            for off, where in ((1, NEW), (0, KEEP)):
                line = bass.AP(dst_line.tensor, off, [[SL, CHAINS], [1, SL + 1]])
                for h in range(HEADS):
                    sp.dma_start(where[h * CHAINS:(h + 1) * CHAINS, :].bitcast(i32), line).then_inc(s_seg, 16)

            def load_xj(i, q):
                sp.wait_ge(s_msg, i * RING + (GROUPS + q + 1))
                sp.dma_start(EA[:, q * GT:(q + 1) * GT, :].rearrange("p k f -> p (k f)"),
                             xj_store[bass.ds(i * RING + q, 1), :, :].rearrange("a p f -> p (a f)")).then_inc(s_ea[q], 16)
            for q in range(RING):
                sp.wait_ge(s_xj[q], 16 * ITERS)
            with sp.Fori(0, ITERS) as i:
                for q in range(RING):
                    load_xj(i, q)

            g3_view = table[3].rearrange("(b p) f -> p b f", p=P)

            def store_g3(c, par):
                sp.wait_ge(s_lrc, c + (CHUNKS + 1))
                sp.dma_start(g3_view[:, bass.ds(c * CB, CB), :], G[:, par * CB:(par + 1) * CB, :]).then_inc(s_lrt[par], 16)
            chunks(sp, store_g3)

            sp.wait_ge(s_x1, CHUNKS)
            sp.dma_start(out[0:(NB - 1) * P, :].rearrange("(b p) f -> p b f", p=P), X[:, 0:NB - 1, :]).then_inc(s_out, 16)
            sp.dma_start(out[(NB - 1) * P:N, :], X[0:REST, NB - 1, :]).then_inc(s_out, 16)
            sp.wait_ge(s_out, 32)

        @block.gpsimd
        def _(pool):
            nc.gpsimd.memset(dst_raw, N)
            nc.gpsimd.memset(src_raw, 0)
            nc.gpsimd.memset(ends[:, 0:1], -1)
            nc.gpsimd.memset(ends[:, 1:2], N + 1)
            nc.gpsimd.memset(X[:, NB - 1:NBP, :], 0.0)
            nc.gpsimd.memset(ones[:], 1.0)
            nc.gpsimd.memset(consts[:, 0:1], LN_EPS)
            nc.gpsimd.memset(consts[:, 1:2], 1.0)
            nc.gpsimd.memset(att4[:], 0.0)
            nc.gpsimd.iota(iota_row[:], [[1, P]], base=0, channel_multiplier=0, allow_small_or_imprecise_dtypes=True)
            nc.gpsimd.memset(AD[:], 0.0)
            nc.gpsimd.memset(HT[:], 0.0)
            nc.gpsimd.memset(ident[:], 0.0).then_inc(s_pre, 1)
            pool.wait_ge(s_pre, 1)
            nc.gpsimd.affine_select(out=ident[:], in_=ident[:], compare_op=ALU.not_equal, fill=1.0, base=0,
                                    pattern=[[-1, P]], channel_multiplier=1).then_inc(s_pre, 1)

            def gather(n, before, ready):
                for s, value in ready:
                    pool.wait_ge(s, value)
                with pool.Fori(0, ITERS) as i:
                    for q in range(RING):
                        before(i, q)
                        pool.wait_ge(s_idx, i * RING + (n * GROUPS + q + 1))
                        settle(pool)
                        for k in range(GT):
                            slot = q * GT + k
                            nc.gpsimd.indirect_dma_start(
                                G[:, slot, :], None, table[n],
                                bass.IndirectOffsetOnAxis(IDX[:, slot:slot + 1], 0)).then_inc(s_gath[q], 16)

            gather(G0, lambda i, q: pool.wait_ge(s_msg, i * RING + (q + 1)), [(s_tab, 16 * CHUNKS)])
            gather(G1, lambda i, q: pool.wait_ge(s_mm, mm(i * RING + (q - RING + A1 * GROUPS))), [(s_tab, 32 * CHUNKS)])

            def attention_slot(i, q):
                pool.wait_ge(s_xj[q], i * 16)
                pool.wait_ge(s_el, i * RING + (q + 1))
            gather(GA, attention_slot, [(s_lrt[par], lr_stored(par)) for par in range(2)])

            pool.wait_ge(s_alc, -(-SEG // GT))
            with pool.Fori(0, ITERS) as i:
                for q in range(RING):
                    b = q % 2
                    pool.wait_ge(s_mm, mm(i * RING + (q - 2 + AB * GROUPS)))
                    pool.wait_ge(s_ea[q], i * 16 + (ea_before(q) + 16))
                    weight = EL[:, bass.ds(i * (RING * GT) + q * GT, GT), :].rearrange("p k h -> p (k h)").unsqueeze(2).to_broadcast([P, GT * HEADS, HF])
                    nc.gpsimd.tensor_tensor(MSG[:, b * GT:(b + 1) * GT, :].rearrange("p k (h f) -> p (k h) f", h=HEADS),
                                            EA[:, q * GT:(q + 1) * GT, :].rearrange("p k (h f) -> p (k h) f", h=HEADS),
                                            weight, ALU.mult).then_inc(s_msg, 1)

            gather(G3, lambda i, q: pool.wait_ge(s_mm, mm(i * RING + (q - RING + A3 * GROUPS))), [(s_lrt[par], g3_stored(par)) for par in range(2)])

        @block.scalar
        def _(act):
            chain = Chain(act, s_achain)
            act.sem_inc(s_el, CREDIT)

            def indices(n, i, q):
                act.wait_ge(s_gath[q], i * (16 * GT) + 16 * GT * n * ITERS)
                nc.scalar.copy(IDX[:, q * GT:(q + 1) * GT], SRC[:, bass.ds(i * (RING * GT) + q * GT, GT)]).then_inc(s_idx, 1)

            def turns(n, body, peel=0):
                for q in range(RING):
                    indices(n, 0, q)
                for i in range(peel):
                    for q in range(RING):
                        body(i, q)
                        indices(n, i + 1, q)
                with act.Fori(peel, ITERS - 1) as i:
                    for q in range(RING):
                        body(i, q)
                        indices(n, i + 1, q)
                for q in range(RING):
                    body(ITERS - 1, q)

            def norm_rows(n):
                act.wait_ge(s_var, (n + 1) * CHUNKS)
                nc.scalar.activation(SD[:], VAR[:], ACT.Sqrt, bias=consts[:, 0:1]).then_inc(s_sd, 1)
                act.wait_ge(s_ln, n + 1)
                if n:
                    act.wait_ge(s_tab, 16 * CHUNKS * min(n, 2))

                def one(c, _):
                    for k in range(CB):
                        last = nc.scalar.activation(
                            H[:, bass.ds(c * CB + k, 1), :].rearrange("p a f -> p (a f)"),
                            X[:, bass.ds(c * CB + k, 1), :].rearrange("p a f -> p (a f)"),
                            ACT.Relu, bias=NM[:, bass.ds(c * CB + k, 1)], scale=RS[:, bass.ds(c * CB + k, 1)])
                    last.then_inc(s_h, 1)
                chunks(act, one)

            def copy_ht(n):
                def one(c, par):
                    act.wait_ge(s_tp, c + (n * CHUNKS + 1))
                    nc.scalar.copy(wide(HT, c), PS[:, par, :]).then_inc(s_ht, 1)
                chunks(act, one)

            def hidden_chunk(n, bias, c, par):
                act.wait_ge(s_m1, c + (n * CHUNKS + 1))
                nc.scalar.activation(MSG[:, par * GT:(par + 1) * GT, :].rearrange("p k f -> p (k f)"), PS[:, 4 + par, :],
                                     ACT.Relu, bias=cols[:, bias:bias + 1]).then_inc(s_z, 1)

            act.wait_ge(s_pre, 2)
            norm_rows(0)
            act.wait_ge(s_ix, 2)

            def rectify(i, q):
                act.wait_ge(s_msg, i * RING + (CREDIT + q + 1))
                m = MSG[:, (q % 2) * GT:(q % 2 + 1) * GT, :]
                nc.scalar.activation(m, m, ACT.Relu).then_inc(s_relu, 1)
            turns(G0, rectify)
            chunks(act, lambda c, par: hidden_chunk(0, B01, c, par))

            norm_rows(1)
            copy_ht(1)
            turns(G1, lambda i, q: None)
            def output1(c, par):
                hidden_chunk(1, B11, c, par)
                act.wait_ge(s_yp, c + 1)
                nc.scalar.activation(wide(ACC, c), PS[:, 6 + par, :], ACT.Identity, bias=cols[:, B02:B02 + 1]).then_inc(s_y, 1)
            chunks(act, output1)
            act.wait_ge(s_bva, 1)
            nc.scalar.activation(small[:, 4:5], small[:, 4:5], ACT.Sqrt).then_inc(s_bsd, 1)
            nc.scalar.activation(DEG, DEG, ACT.Sqrt, bias=consts[:, 1:2]).then_inc(s_dsd, 1)
            act.wait_ge(s_bns, 1)

            def batch_norm(c, _):
                nc.scalar.activation(wide(ACC, c), wide(ACC, c), ACT.Identity, bias=small[:, 3:4], scale=small[:, 2:3]).then_inc(s_bn, 1)
            chunks(act, batch_norm)

            norm_rows(2)
            copy_ht(2)

            def stage_lr(c, par):
                act.wait_ge(s_lrp, c + 1)
                nc.scalar.copy(EA[:, par * CB:(par + 1) * CB, :].rearrange("p (b s) f -> p b s f", s=2),
                               PS[:, 4 + 2 * par:6 + 2 * par, :].rearrange("p b (s w f) -> p b w s f", s=2, w=2)[:, :, 0])
                nc.scalar.copy(G[:, par * CB:(par + 1) * CB, :].rearrange("p (b s) f -> p b s f", s=2),
                               PS[:, 4 + 2 * par:6 + 2 * par, :].rearrange("p b (s w f) -> p b w s f", s=2, w=2)[:, :, 1]).then_inc(s_lrc, 1)

            stage_lr(0, 0)
            stage_lr(1, 1)
            with act.Fori(1, CHUNKS // 2) as j:
                for par in range(2):
                    act.wait_ge(s_lrt[par], j * 32)
                    stage_lr(2 * j + par, par)
            act.wait_ge(s_lrt[0], CHUNKS // 2 * 32)
            stage_lr(CHUNKS - 1, 0)

            def copy_oht(i, q):
                b = q % 2
                act.wait_ge(s_ohtp, i * RING + (q + 1))
                nc.scalar.copy(OHT[:, b * GT:(b + 1) * GT, :].rearrange("p k f -> p (k f)"), PS[:, b, :]).then_inc(s_oht, 1)

            def copy_logits(i, q):
                b = q % 2
                act.wait_ge(s_lg, i * RING + (q + 1))
                nc.scalar.copy(EL[:, bass.ds(i * (RING * GT) + q * GT, GT), :],
                               PS[:, 4 + b, 0:GT * HEADS].rearrange("p (k h) -> p k h", h=HEADS)).then_inc(s_el, 1)

            def attend(i, q):
                if q < RING - 1:
                    copy_oht(i, q + 1)
                elif not isinstance(i, int) or i < ITERS - 1:
                    copy_oht(i + 1, 0)
                b = q % 2
                act.wait_ge(s_zz, i * RING + (q + 1))
                nc.scalar.mul(MSG[:, b * GT:(b + 1) * GT, :].rearrange("p k f -> p (k f)"), PS[:, 2 + b, :], SLOPE).then_inc(s_sl, 1)
                if q > 0:
                    copy_logits(i, q - 1)
                elif not isinstance(i, int) or i > 0:
                    copy_logits(i - 1, RING - 1)
            copy_oht(0, 0)
            turns(GA, attend, 1)
            copy_logits(ITERS - 1, RING - 1)

            for n, g in enumerate(range(0, SEG, GT)):
                w = min(GT, SEG - g)
                act.wait_ge(s_sc, n + 1)
                nc.scalar.copy(S[:, g * P:(g + w) * P], PS[:, n % 2, 0:w * P]).then_inc(s_scc, 1)
            act.wait_ge(s_sub, 1)
            nc.scalar.activation(S, S, ACT.Exp).then_inc(s_exp, 1)

            norm_rows(3)
            def stage_g3(c, par):
                nc.scalar.copy(G[:, par * CB:(par + 1) * CB, :].rearrange("p k f -> p (k f)"), PS[:, 4 + par, :]).then_inc(s_lrc, 1)
                nc.scalar.copy(wide(ACC, c), PS[:, 6 + par, :]).then_inc(s_ht, 1)
            for c in (0, 1):
                act.wait_ge(s_lrp, CHUNKS + c + 1)
                stage_g3(c, c)
            with act.Fori(1, CHUNKS // 2) as j:
                for par in range(2):
                    act.wait_ge(s_lrt[par], j * 16 + lr_stored(par))
                    act.wait_ge(s_lrp, j * 2 + (par + CHUNKS + 1))
                    stage_g3(2 * j + par, par)
            act.wait_ge(s_lrt[0], CHUNKS // 2 * 16 + lr_stored(0))
            act.wait_ge(s_lrp, 2 * CHUNKS)
            stage_g3(CHUNKS - 1, 0)
            turns(G3, lambda i, q: None)

            def hidden3(c, par):
                act.wait_ge(s_dv, c + 1)
                nc.scalar.activation(MSG[:, par * GT:(par + 1) * GT, :], MSG[:, par * GT:(par + 1) * GT, :],
                                     ACT.Relu, bias=cols[:, B3:B3 + 1]).then_inc(s_z, 1)
            chunks(act, hidden3)

        @block.vector
        def _(dve):
            chain = Chain(dve, s_chain)
            dve.sem_inc(s_msg, CREDIT)
            dve.sem_inc(s_add, GT * CREDIT)

            dve.wait_ge(s_raw, 16 * 6)
            nc.vector.tensor_copy(src_f, src_raw)
            chain.one(nc.vector.tensor_copy(dst_f, dst_raw))
            nc.vector.tensor_tensor(loc_f, dst_f, dst_f[:, :, 0:1].to_broadcast([P, TG, P]), ALU.subtract).then_inc(s_f, 1)
            dve.wait_ge(s_tp0, 1)
            nc.vector.tensor_copy(SRC[:], PS[:, 0:2, :].rearrange("p b f -> p (b f)")[:, 0:T])
            nc.vector.tensor_copy(LD[:], PS[:, 2:4, :].rearrange("p b f -> p (b f)")[:, 0:T])
            nc.vector.tensor_copy(WIN[:], PS[0:1, 4:6, :].rearrange("p b f -> p (b f)")[:, 0:T]).then_inc(s_ix, 1)
            dve.wait_ge(s_w, 16 * 18)
            dve.wait_ge(s_pre, 2)
            chain.one(nc.vector.tensor_scalar(cols[:, E1:E1 + 1], cols[:, E1:E1 + 1], 1.0, None, ALU.add))
            for h in range(HEADS):
                last = nc.vector.tensor_copy(att4[h * HF:(h + 1) * HF, h:h + 1], cols[h * HF:(h + 1) * HF, ATT:ATT + 1])
            chain.one(last)
            dve.wait_ge(s_tp0, 2)
            chain.one(nc.vector.tensor_copy(W["ln"][:], PS[:, 6, 0:P]))
            nc.vector.memset(small[:, 7:8], 0.0).then_inc(s_ix, 1)

            NORM_LINKS = 2

            def norm_stats(c, par):
                settle(dve)
                for k in range(CB):
                    last = nc.vector.bn_stats(ST[:, par * CB + k, :], X[:, bass.ds(c * CB + k, 1), :].rearrange("p a f -> p (a f)"))
                chain.link(last)
                settle(dve)
                for k in range(CB):
                    last = nc.vector.bn_aggr(MV[:, par * CB + k, :], ST[:, par * CB + k, :])
                chain.link(last)
                nc.vector.tensor_copy(MEAN[:, bass.ds(c * CB, CB)], MV[:, par * CB:(par + 1) * CB, 0])
                return nc.vector.tensor_copy(VAR[:, bass.ds(c * CB, CB)], MV[:, par * CB:(par + 1) * CB, 1])

            def norm_scales(n):
                dve.wait_ge(s_sd, n + 1)
                chain.one(nc.vector.reciprocal(RS[:], SD[:]))
                nc.vector.scalar_tensor_tensor(NM[:], MEAN[:], -1.0, RS[:], ALU.mult, ALU.mult).then_inc(s_ln, 1)

            dve.wait_ge(s_x, 32)

            def first_norm(c, par):
                chain.at(c, NORM_LINKS)
                norm_stats(c, par).then_inc(s_var, 1)
            chunks(dve, first_norm)
            chain.done(CHUNKS, NORM_LINKS)
            norm_scales(0)

            def start0(c, par):
                dve.wait_ge(s_tp, c + 1)
                nc.vector.tensor_scalar(wide(ACC, c), PS[:, par, :], cols[:, E1:E1 + 1], None, ALU.mult).then_inc(s_acc0, 1)
            chunks(dve, start0)

            iota_b = iota_row[:].unsqueeze(1).to_broadcast([P, GT, P])

            def onehot(i, q, a):
                b = q % 2
                where = LD[:, bass.ds(i * (RING * GT) + q * GT, GT)].unsqueeze(2).to_broadcast([P, GT, P])
                nc.vector.tensor_tensor(OH[:, b * GT:(b + 1) * GT, :], iota_b, where, ALU.is_equal).then_inc(s_oh, 1)

            def add(i, q, a, starts, degrees=False):
                b = q % 2
                first = i * (RING * GT) + q * GT
                dve.wait_ge(s_mm, mm(i * RING + (q + a * GROUPS)))
                for k in range(GT):
                    dve.wait_ge(s_add, first + (a * T + GT * CREDIT + k - (a == AB)))
                    if degrees:
                        w = AD[:, :, bass.ds(starts[q * GT + k], P)]
                        nc.vector.tensor_tensor(w, w, PS[:, 2 * b:2 * b + 2, k * P:(k + 1) * P], ALU.add).then_inc(s_add, 1)
                    else:
                        to = HT if a == AB and k % 2 else ACC
                        w = to[:, bass.ds(starts[q * GT + k], P)]
                        nc.vector.tensor_tensor(w, w, PS[:, 2 * b, k * P:(k + 1) * P], ALU.add).then_inc(s_add, 1)

            def turns(produce, consume, lead=1):
                for q in range(lead):
                    produce(0, q)
                with dve.Fori(0, ITERS - 1) as i:
                    starts = window_starts(mybir.EngineType.DVE, i)
                    for q in range(RING):
                        produce(*((i, q + lead) if q + lead < RING else (i + 1, q + lead - RING)))
                        consume(i, q, starts)
                starts = window_starts(mybir.EngineType.DVE, ITERS - 1)
                for q in range(RING):
                    if q + lead < RING:
                        produce(ITERS - 1, q + lead)
                    consume(ITERS - 1, q, starts)

            def free2(i, q, a):
                dve.wait_ge(s_mm, mm(i * RING + (q - 2 + a * GROUPS)))

            def message0(i, q):
                b = q % 2
                free2(i, q, A0)
                dve.wait_ge(s_gath[q], i * (16 * GT) + 16 * GT)
                extra = 16 if q == (tail_slot // GT) and isinstance(i, int) and i == ITERS - 1 else 0
                dve.wait_ge(s_ea[q], i * 16 + (16 + extra))
                nc.vector.tensor_tensor(MSG[:, b * GT:(b + 1) * GT, :], G[:, q * GT:(q + 1) * GT, :],
                                        EA[:, q * GT:(q + 1) * GT, :], ALU.add).then_inc(s_msg, 1)
                onehot(i, q, A0)
            turns(message0, lambda i, q, starts: add(i, q, A0, starts))

            def rows_and_norm(n, norm=True):
                links = NORM_LINKS + 1

                def one(c, par):
                    chain.at(c, links)
                    dve.wait_ge(s_m2, c + (n * CHUNKS + 1))
                    ins = nc.vector.tensor_tensor(nodes(X, c).rearrange("p b f -> p (b f)"),
                                                  nodes(X, c).rearrange("p b f -> p (b f)"), PS[:, 6 + par if n != 1 else 4 + par, :], ALU.add)
                    chain.link(ins)
                    norm_stats(c, par).then_inc(s_var, 1)
                chunks(dve, one)
                chain.done(CHUNKS, links)
                norm_scales(n + 1)

            rows_and_norm(0)

            def start1(c, _):
                dve.wait_ge(s_ht, c + 1)
                nc.vector.tensor_copy(wide(ACC, c), wide(HT, c)).then_inc(s_acc0, 1)
            chunks(dve, start1)

            def produce1(i, q):
                free2(i, q, A1)
                onehot(i, q, A1)
            turns(produce1, lambda i, q, starts: add(i, q, A1, starts, degrees=True))

            for c in range(CHUNKS):
                n0 = c * CB * P
                w = min(CB * P, N - n0)
                dve.wait_ge(s_y, c + 1)
                last = nc.vector.bn_stats(ST[:, c, :], ACC[:, n0:n0 + w])
            chain.one(last)
            chain.one(nc.vector.bn_aggr(small[:, 0:2], ST[:, 0:CHUNKS, :].rearrange("p c s -> p (c s)")))
            nc.vector.tensor_scalar(small[:, 4:5], small[:, 1:2], BN_EPS, None, ALU.add).then_inc(s_bva, 1)
            dve.wait_ge(s_bsd, 1)
            chain.one(nc.vector.reciprocal(small[:, 4:5], small[:, 4:5]))
            chain.one(nc.vector.tensor_tensor(small[:, 2:3], small[:, 4:5], cols[:, GAM:GAM + 1], ALU.mult))
            chain.one(nc.vector.tensor_tensor(small[:, 5:6], small[:, 0:1], small[:, 2:3], ALU.mult))
            nc.vector.tensor_tensor(small[:, 3:4], cols[:, BET:BET + 1], small[:, 5:6], ALU.subtract).then_inc(s_bns, 1)
            rows_and_norm(1)
            dve.wait_ge(s_dsd, 1)
            chain.one(nc.vector.reciprocal(DEG, DEG))

            def produce_a(i, q):
                dve.wait_ge(s_ohtp, i * RING + (q + 1 - 2)) if (isinstance(i, int) and i * RING + q >= 2) or not isinstance(i, int) else None
                onehot(i, q, 2)

            def leaky(i, q, _):
                b = q % 2
                dve.wait_ge(s_sl, i * RING + (q + 1))
                m = MSG[:, b * GT:(b + 1) * GT, :].rearrange("p k f -> p (k f)")
                nc.vector.tensor_tensor(m, m, PS[:, 2 + b, :], ALU.max).then_inc(s_lk, 1)
            turns(produce_a, leaky, 2)

            el_view = EL[:].rearrange("p (j g) h -> p g h j", g=SEG)
            dve.wait_ge(s_el, GROUPS + CREDIT)
            nc.vector.tensor_copy(F.rearrange("p (g h j) -> p g h j", g=SEG, h=HEADS), el_view).then_inc(s_sort, 1)
            dve.wait_ge(s_seg, 16 * 2 * HEADS)
            new_i, keep_i = NEW.bitcast(i32), KEEP.bitcast(i32)
            chain.one(nc.vector.tensor_tensor(NEW, new_i, keep_i, ALU.not_equal))
            chain.one(nc.vector.tensor_scalar(KEEP, NEW, -1.0, 1.0, ALU.mult, ALU.add))
            chain.one(nc.vector.tensor_scalar(NEW, NEW, -BIG, None, ALU.mult))
            dve.wait_ge(s_scc, -(-SEG // GT))
            resolved = [0]
            local = H[:, 0:SEG, :].rearrange("p b f -> p (b f)")

            def scan(gate, data, join, outward, backward, initial):
                turn = (lambda ap: ap[:, ::-1]) if backward else (lambda ap: ap)
                chain.one(nc.vector.tensor_tensor_scan(turn(local), turn(gate), turn(data), initial, outward, join))
                end = local[:, 0:1] if backward else local[:, SL - 1:SL]
                nc.vector.tensor_copy(small[:, 0:1], end)
                nc.vector.tensor_reduce(small[:, 1:2], gate, AX.X, ALU.min).then_inc(s_cr, 1)
                resolved[0] += 1
                dve.wait_ge(s_crt, resolved[0])
                nc.vector.memset(carry[:], initial)
                chain.one(nc.vector.tensor_copy(carry_rows[:], PS[0:1, 6, 0:2 * P]))
                for h in range(HEADS):
                    data_h = carry_rows[0:1, h * CHAINS:(h + 1) * CHAINS]
                    gate_h = carry_rows[0:1, P + h * CHAINS:P + (h + 1) * CHAINS]
                    to = carry[0:1, h, 0:CHAINS] if backward else carry[0:1, h, 1:CHAINS + 1]
                    last = nc.vector.tensor_tensor_scan(turn(to), turn(gate_h), turn(data_h), initial, outward, join)
                chain.one(last)
                nc.vector.tensor_copy(carry_rows[:, 0:P].rearrange("p (h j) -> p h j", h=HEADS),
                                      carry[:, :, 1:CHAINS + 1] if backward else carry[:, :, 0:CHAINS]).then_inc(s_ci, 1)
                dve.wait_ge(s_cit, resolved[0])
                chain.one(nc.vector.tensor_copy(small[:, 2:3], PS[:, 7, 0:1]))
                return turn, gate, data, small[:, 2:3], outward, join

            def finish(to, turn, gate, data, first, outward, join):
                chain.one(nc.vector.tensor_tensor_scan(turn(to), turn(gate), turn(data), first, outward, join))

            ahead, behind = NEW[:, 1:SL + 1], NEW[:, 0:SL]
            finish(F, *scan(behind, S, ALU.max, ALU.add, False, -BIG))
            finish(F, *scan(ahead, F, ALU.max, ALU.add, True, -BIG))
            nc.vector.tensor_tensor(S, S, F, ALU.subtract).then_inc(s_sub, 1)
            dve.wait_ge(s_exp, 1)
            finish(F, *scan(KEEP[:, 0:SL], S, ALU.add, ALU.mult, False, 0.0))
            finish(F, *scan(ahead, F, ALU.max, ALU.add, True, -BIG))
            chain.one(nc.vector.tensor_scalar(F, F, 1e-16, None, ALU.max))
            chain.one(nc.vector.reciprocal(F, F))
            nc.vector.tensor_tensor(S, S, F, ALU.mult).then_inc(s_al, 1)
            chain.one(nc.vector.memset(ACC, 0.0))
            for n, g in enumerate(range(0, SEG, GT)):
                w = min(GT, SEG - g)
                dve.wait_ge(s_alt, n + 1)
                last = nc.vector.tensor_copy(el_view[:, g:g + w], PS[:, n % 2, 0:w * P].rearrange("p (g h j) -> p g h j", g=w, h=HEADS))
                last.then_inc(s_alc, 1)
            dve.wait_ge(s_alc, -(-SEG // GT))
            nc.vector.memset(HT[:], 0.0).then_inc(s_az, 1)
            dve.wait_ge(s_az, 1)

            def message_b(i, q):
                free2(i, q, AB)
                onehot(i, q, 3)
            turns(message_b, lambda i, q, starts: add(i, q, AB, starts))
            rows_and_norm(2)

            def scale3(c, par):
                dve.wait_ge(s_tp, c + (3 * CHUNKS + 1))
                nc.vector.tensor_tensor(wide(HT, c), PS[:, par, :], wide(DEG, c), ALU.mult).then_inc(s_acc0, 1)
            chunks(dve, scale3)

            def produce3(i, q):
                free2(i, q, A3)
                onehot(i, q, 4)
            dve.wait_ge(s_ht, 3 * CHUNKS)
            turns(produce3, lambda i, q, starts: add(i, q, A3, starts))
            dve.wait_ge(s_add, added(4 * GROUPS - 1))

            def times_dinv(c, par):
                nc.vector.tensor_tensor(MSG[:, par * GT:(par + 1) * GT, :].rearrange("p k f -> p (k f)"),
                                        wide(ACC, c), wide(DEG, c), ALU.mult).then_inc(s_dv, 1)
            links = 1

            def last_rows(c, par):
                chain.at(c, links)
                times_dinv(c, par)
                dve.wait_ge(s_m2, c + (3 * CHUNKS + 1))
                h, xr = (nodes(v, c).rearrange("p b f -> p (b f)") for v in (H, X))
                chain.link(nc.vector.tensor_tensor(h, h, PS[:, 6 + par, :], ALU.add))
                nc.vector.scalar_tensor_tensor(xr, h, 0.0, xr, ALU.max, ALU.add).then_inc(s_x1, 1)
            chunks(dve, last_rows)
            chain.done(CHUNKS, links)

        @block.tensor
        def _(pe):
            pe.sem_inc(s_mm, CREDIT)
            pe.wait_ge(s_pre, 2)
            pe.wait_ge(s_f, 1)
            for g in range(TG):
                cols_g = min(P, T - g * P)
                bank, off = divmod(g * P, GT * P)
                nc.tensor.transpose(PS[:, bank, off:off + P], src_f[:, g, :], ident[:])
                nc.tensor.transpose(PS[:, 2 + bank, off:off + P], loc_f[:, g, :], ident[:])
                last = nc.tensor.transpose(PS[0:1, 4 + bank, off:off + P], dst_f[:, g, 0:1], ident[:])
            last.then_inc(s_tp0, 1)
            pe.wait_ge(s_w, 16 * 18)
            nc.tensor.transpose(PS[:, 6, 0:P], W["ln_raw"][:], ident[:]).then_inc(s_tp0, 1)
            pe.wait_ge(s_ix, 2)

            def block_of(buf, c, k):
                at = (c * CB + k) * P
                return buf[:, at:at + P]

            def transpose_h(n, taken, per):
                for c in range(CHUNKS):
                    pe.wait_ge(s_h, n * CHUNKS + c + 1)
                    if c >= 2:
                        for s, before in taken:
                            pe.wait_ge(s, before + c - 1)
                    for k in range(CB):
                        last = nc.tensor.transpose(PS[:, c % 2, k * P:(k + 1) * P], H[:, c * CB + k, :], ident[:])
                    last.then_inc(s_tp, 1)

            def aggregate(a, ready, degrees=False, rows_of=lambda q: (MSG, (q % 2) * GT)):
                with pe.Fori(0, ITERS) as i:
                    for q in range(RING):
                        b = q % 2
                        pe.wait_ge(s_add, added(i * RING + (q - 2 + a * GROUPS)))
                        ready(i, q)
                        buf, at = rows_of(q)
                        for k in range(GT):
                            last = nc.tensor.matmul(PS[:, 2 * b, k * P:(k + 1) * P], buf[:, at + k, :], OH[:, b * GT + k, :],
                                                    start=True, stop=True)
                        if degrees:
                            last = nc.tensor.matmul(PS[:, 2 * b + 1, :], ones[:], OH[:, b * GT:(b + 1) * GT, :].rearrange("p k f -> p (k f)"),
                                                    start=True, stop=True)
                        last.then_inc(s_mm, 1)

            def ohs(n, i, q):
                pe.wait_ge(s_oh, i * RING + (n * GROUPS + q + 1))

            transpose_h(0, [(s_acc0, 0)], 1)
            pe.wait_ge(s_acc0, CHUNKS)

            def ready0(i, q):
                ohs(0, i, q)
                pe.wait_ge(s_relu, i * RING + (q + 1))
            aggregate(A0, ready0)

            def perceptron_in(n, w):
                def one(c):
                    if c >= 2:
                        pe.wait_ge(s_z, n * CHUNKS + c - 1)
                    nc.tensor.matmul(PS[:, 4 + c % 2, :], W[w][:], ACC[:, c * CB * P:(c + 1) * CB * P], start=True, stop=True).then_inc(s_m1, 1)
                return one

            def bias_rows(bank, which, stop=False):
                nc.tensor.matmul(PS[:, bank, :].rearrange("p (k f) -> p k f", f=P), ones[0:1, :], rows[0:1, which, :].unsqueeze(1).to_broadcast([1, CB, P]),
                                 start=True, stop=stop)

            pe.wait_ge(s_add, added(GROUPS - 1))
            first = perceptron_in(0, "g0_1")
            first(0)
            for c in range(CHUNKS):
                if c + 1 < CHUNKS:
                    first(c + 1)
                pe.wait_ge(s_z, c + 1)
                if c >= 2:
                    pe.wait_ge(s_var, CHUNKS + c - 1)
                bias_rows(6 + c % 2, 0)
                for k in range(CB):
                    last = nc.tensor.matmul(PS[:, 6 + c % 2, k * P:(k + 1) * P], MSG[:, (c % 2) * GT + k, :], W["g0_2"][:],
                                            start=False, stop=k == CB - 1)
                last.then_inc(s_m2, 1)

            transpose_h(1, [(s_ht, 0)], 1)
            pe.wait_ge(s_acc0, 2 * CHUNKS)
            pe.wait_ge(s_ht, CHUNKS)

            def ready1(i, q):
                ohs(1, i, q)
                pe.wait_ge(s_gath[q], i * (16 * GT) + 16 * GT * (G1 * ITERS + 1))
            aggregate(A1, ready1, True, lambda q: (G, q * GT))

            pe.wait_ge(s_add, added(2 * GROUPS - 1))
            first = perceptron_in(1, "g1_1")
            first(0)
            for c in range(CHUNKS):
                if c + 1 < CHUNKS:
                    first(c + 1)
                pe.wait_ge(s_z, CHUNKS + c + 1)
                if c >= 2:
                    pe.wait_ge(s_y, c - 1)
                nc.tensor.matmul(PS[:, 6 + c % 2, :], W["g1_2"][:], MSG[:, (c % 2) * GT:(c % 2 + 1) * GT, :].rearrange("p k f -> p (k f)"),
                                 start=True, stop=True).then_inc(s_yp, 1)
            for c in range(CHUNKS):
                pe.wait_ge(s_bn, c + 1)
                if c >= 2:
                    pe.wait_ge(s_var, 2 * CHUNKS + c - 1)
                for k in range(CB):
                    to = PS[:, 4 + c % 2, k * P:(k + 1) * P]
                    nc.tensor.matmul(to, block_of(ACC, c, k), ident[:], start=True, stop=False)
                    last = nc.tensor.matmul(to, block_of(HT, c, k), ident[:], start=False, stop=True)
                last.then_inc(s_m2, 1)

            transpose_h(2, [(s_ht, CHUNKS)], 1)
            for c in range(CHUNKS):
                pe.wait_ge(s_ht, CHUNKS + c + 1)
                if c >= 2:
                    pe.wait_ge(s_lrc, c - 1)
                for k in range(CB):
                    last = nc.tensor.matmul(PS[:, 4 + 2 * (c % 2) + k // 2, (k % 2) * 2 * P:(k % 2 + 1) * 2 * P],
                                            block_of(HT, c, k), WLR[:], start=True, stop=True)
                last.then_inc(s_lrp, 1)

            pe.wait_ge(s_lrc, CHUNKS)

            def flip(i, q):
                b = q % 2
                ohs(2, i, q)
                if not (isinstance(i, int) and i * RING + q < 2):
                    pe.wait_ge(s_oht, i * RING + (q + 1 - 2))
                for k in range(GT):
                    last = nc.tensor.transpose(PS[:, b, k * P:(k + 1) * P], OH[:, b * GT + k, :], ident[:])
                last.then_inc(s_ohtp, 1)

            def sums(i, q):
                b = q % 2
                pe.wait_ge(s_oht, i * RING + (q + 1))
                pe.wait_ge(s_ea[q], i * (16 * GT) + (16 * ITERS + (16 if q == (tail_slot // GT) else 0) + 16 * GT))
                pe.wait_ge(s_gath[q], i * (16 * GT) + 16 * GT * (GA * ITERS + 1))
                if not (isinstance(i, int) and i * RING + q < 2):
                    pe.wait_ge(s_lk, i * RING + (q + 1 - 2))
                for k in range(GT):
                    to = PS[:, 2 + b, k * P:(k + 1) * P]
                    nc.tensor.matmul(to, EA[:, q * GT + k, :], OHT[:, b * GT + k, :], start=True, stop=False)
                    last = nc.tensor.matmul(to, G[:, q * GT + k, :], ident[:], start=False, stop=True)
                last.then_inc(s_zz, 1)

            def logits(i, q):
                b = q % 2
                pe.wait_ge(s_lk, i * RING + (q + 1))
                pe.wait_ge(s_el, i * RING + (q + 1 + CREDIT - 2))
                for k in range(GT):
                    last = nc.tensor.matmul(PS[:, 4 + b, k * HEADS:(k + 1) * HEADS], MSG[:, b * GT + k, :], att4[:], start=True, stop=True)
                last.then_inc(s_lg, 1)

            def attend(i, q):
                if q < RING - 1:
                    flip(i, q + 1)
                elif not isinstance(i, int) or i < ITERS - 1:
                    flip(i + 1, 0)
                sums(i, q)
                if q > 0:
                    logits(i, q - 1)
                elif not isinstance(i, int) or i > 0:
                    logits(i - 1, RING - 1)
            flip(0, 0)
            for q in range(RING):
                attend(0, q)
            with pe.Fori(1, ITERS - 1) as i:
                for q in range(RING):
                    attend(i, q)
            for q in range(RING):
                attend(ITERS - 1, q)
            logits(ITERS - 1, RING - 1)

            pe.wait_ge(s_sort, 1)
            for n, g in enumerate(range(0, SEG, GT)):
                if n >= 2:
                    pe.wait_ge(s_scc, n - 1)
                for k in range(min(GT, SEG - g)):
                    last = nc.tensor.transpose(PS[:, n % 2, k * P:(k + 1) * P], F[:, (g + k) * P:(g + k + 1) * P], ident[:])
                last.then_inc(s_sc, 1)

            for n in range(4):
                pe.wait_ge(s_cr, n + 1)
                nc.tensor.transpose(PS[0:1, 6, 0:P], small[:, 0:1], ident[:])
                nc.tensor.transpose(PS[0:1, 6, P:2 * P], small[:, 1:2], ident[:]).then_inc(s_crt, 1)
                pe.wait_ge(s_ci, n + 1)
                nc.tensor.transpose(PS[:, 7, 0:1], carry_rows[:, 0:P], ident[0:1, 0:1]).then_inc(s_cit, 1)

            pe.wait_ge(s_al, 1)
            for n, g in enumerate(range(0, SEG, GT)):
                if n >= 2:
                    pe.wait_ge(s_alc, n - 1)
                for k in range(min(GT, SEG - g)):
                    last = nc.tensor.transpose(PS[:, n % 2, k * P:(k + 1) * P], S[:, (g + k) * P:(g + k + 1) * P], ident[:])
                last.then_inc(s_alt, 1)

            pe.wait_ge(s_alc, -(-SEG // GT))

            def ready_b(i, q):
                ohs(3, i, q)
                pe.wait_ge(s_msg, i * RING + (GROUPS + CREDIT + q + 1))
            aggregate(AB, ready_b)

            pe.wait_ge(s_add, added(3 * GROUPS - 1))
            for c in range(CHUNKS):
                if c >= 2:
                    pe.wait_ge(s_var, 3 * CHUNKS + c - 1)
                bias_rows(6 + c % 2, 1)
                for k in range(CB):
                    to = PS[:, 6 + c % 2, k * P:(k + 1) * P]
                    nc.tensor.matmul(to, block_of(ACC, c, k), ident[:], start=False, stop=False)
                    last = nc.tensor.matmul(to, block_of(HT, c, k), ident[:], start=False, stop=k == CB - 1)
                last.then_inc(s_m2, 1)

            transpose_h(3, [(s_acc0, 2 * CHUNKS)], 1)
            for c in range(CHUNKS):
                pe.wait_ge(s_acc0, 2 * CHUNKS + c + 1)
                if c >= 2:
                    pe.wait_ge(s_lrc, CHUNKS + c - 1)
                    pe.wait_ge(s_ht, 2 * CHUNKS + c - 1)
                for k in range(CB):
                    nc.tensor.matmul(PS[:, 4 + c % 2, k * P:(k + 1) * P], block_of(HT, c, k), W["g3"][:], start=True, stop=True)
                nc.tensor.matmul(PS[:, 6 + c % 2, :], W["g3"][:], HT[:, c * CB * P:(c + 1) * CB * P], start=True, stop=True).then_inc(s_lrp, 1)

            def ready3(i, q):
                ohs(4, i, q)
                pe.wait_ge(s_gath[q], i * (16 * GT) + 16 * GT * (G3 * ITERS + 1))
            aggregate(A3, ready3, False, lambda q: (G, q * GT))
            for c in range(CHUNKS):
                pe.wait_ge(s_z, 2 * CHUNKS + c + 1)
                if c >= 2:
                    pe.wait_ge(s_x1, c - 1)
                for k in range(CB):
                    last = nc.tensor.matmul(PS[:, 6 + c % 2, k * P:(k + 1) * P], MSG[:, (c % 2) * GT + k, :], W["ln"][:], start=True, stop=True)
                last.then_inc(s_m2, 1)


_INS = ["x", "src", "dst", "edge_attr_128", "L0_gnn_W1", "L0_gnn_b1", "L0_gnn_W2", "L0_gnn_b2", "L0_gnn_eps",
        "L1_gnn_W1", "L1_gnn_b1", "L1_gnn_W2", "L1_gnn_b2", "L1_gnn_gamma", "L1_gnn_beta", "L2_gnn_weight_l",
        "L2_gnn_weight_r", "L2_gnn_att", "L2_gnn_bias", "L3_gnn_W_gcn", "L3_gnn_b_gcn", "L3_gnn_W_ln"]


def kernel(**inputs):
    import numpy as _np
    import concourse.bacc as _bacc
    from concourse import mybir as _mybir
    from concourse.bass_utils import run_bass_kernel_spmd as _run

    nc = _bacc.Bacc("TRN2", target_bir_lowering=False, num_devices=1)
    arrays, args = {}, []
    for name in _INS:
        a = _np.ascontiguousarray(inputs[name])
        arrays[f"in_{name}_dram"] = a
        args.append(nc.dram_tensor(f"in_{name}_dram", a.shape, _mybir.dt.from_np(a.dtype), kind="ExternalInput").ap())
    shape = _np.shape(inputs["x"])
    args.append(nc.dram_tensor("out_0_dram", shape, _mybir.dt.float32, kind="ExternalOutput").ap())
    build(nc, *args)
    r = _run(nc, [arrays], core_ids=[0])
    return r.results[0]["out_0_dram"]
```

```python
from contextlib import ExitStack

import concourse.bass as bass
from concourse import mybir

f32 = mybir.dt.float32
i32 = mybir.dt.int32
ALU = mybir.AluOpType
ACT = mybir.ActivationFunctionType
AX = mybir.AxisListType

P = 128
BIG = 1e30
LN_EPS = 1e-5
BN_EPS = 1e-5
SLOPE = 0.2
HEADS = 4
HF = P // HEADS

GT = 4
RING = 4
CB = 4


class Chain:

    def __init__(self, eng, sem):
        self.eng, self.sem, self.base, self.n = eng, sem, 0, 0

    def at(self, step, per):
        self.n, self.left = step * per + self.base, per

    def done(self, steps, per):
        self.base += steps * per
        self.n = self.base

    def link(self, ins):
        ins.then_inc(self.sem, 1)
        self.n = self.n + 1
        self.eng.wait_ge(self.sem, self.n)

    def one(self, ins):
        self.base += 1
        self.n = self.base
        ins.then_inc(self.sem, 1)
        self.eng.wait_ge(self.sem, self.n)


def build(nc, x, src, dst, edge_attr, g0_w1, g0_b1, g0_w2, g0_b2, g0_eps, g1_w1, g1_b1, g1_w2, g1_b2,
          g1_gamma, g1_beta, g2_wl, g2_wr, g2_att, g2_bias, g3_w, g3_b, g3_wln, out):
    N = x.shape[0]
    E = src.shape[0]
    ITERS = -(-E // (P * GT * RING))
    GROUPS = ITERS * RING
    T = GROUPS * GT
    NB = -(-N // P)
    CHUNKS = -(-(NB + 1) // CB)
    NBP = CHUNKS * CB
    NW = NBP * P
    CHAINS = 32
    SEG = T // CHAINS
    SL = SEG * P
    assert SEG * CHAINS == T and HEADS * CHAINS == P and N + P <= NW and CHUNKS % 2 == 1
    FULL = E // P
    TG = -(-T // P)
    REST = N - (NB - 1) * P

    ctx = ExitStack()
    with ctx:
        def sb(name, shape, dt=f32):
            return ctx.enter_context(nc.sbuf_tensor(name, shape, dt))

        def sem(name):
            return ctx.enter_context(nc.semaphore(name))

        def dram(name, shape, dt=f32):
            return nc.dram_tensor(name, shape, dt, kind="Internal").ap()

        table = [dram(f"table{n}", [NW, P]) for n in range(4)]
        hl_table = dram("hl_table", [NW, P])
        xj_store = dram("xj_store", [GROUPS, P, GT * P])
        sorted_pairs = dram("sorted_pairs", [T * P, 2])
        sorted_ea = dram("sorted_ea", [T * P, P])
        sorted_x = dram("sorted_x", [NW, P])
        dst_line = dram("dst_line", [T * P + 2], i32)

        X = sb("X", [P, NBP, P])
        H = sb("H", [P, NBP, P])
        HT = sb("HT", [P, NW + 4])
        AD = sb("AD", [P, 2, NW + 4])
        ACC, DEG = AD[:, 0, :], AD[:, 1, :]
        SRC = sb("SRC", [P, T])
        LD = sb("LD", [P, T])
        WIN = sb("WIN", [1, T], i32)
        GWIN = sb("GWIN", [1, GROUPS], i32)
        spread = sb("spread", [1, GROUPS])
        away = sb("away", [1, T])
        EA = sb("EA", [P, RING * GT, P])
        G = sb("G", [P, RING * GT, P])
        MSG = sb("MSG", [P, 2 * GT, P])
        OH = sb("OH", [P, RING * GT, P])
        OHT = OH[:, 2 * GT:4 * GT, :]
        EL = sb("EL", [P, T, HEADS])
        IDX = sb("IDX", [P, RING * GT], i32)
        ident = sb("ident", [P, P])
        iota_row = sb("iota_row", [P, P])
        ones = sb("ones", [P, P])
        W = {n: sb("w_" + n, [P, P]) for n in ("g0_1", "g0_2", "g1_1", "g1_2", "g3", "ln_raw", "ln")}
        WLR = sb("w_lr", [P, 2 * P])
        att4 = sb("att4", [P, HEADS])
        cols = sb("cols", [P, 8])
        rows = sb("rows", [P, 2, P])
        ST = sb("ST", [P, max(2 * CB, CHUNKS), 6])
        MV = sb("MV", [P, 2 * CB, 2])
        MVS = sb("MVS", [P, NBP, 2])
        SD, RS, NM = (sb(n, [P, NBP]) for n in ("SD", "RS", "NM"))
        consts = sb("consts", [P, 2])
        small = sb("small", [P, 8])
        carry_rows = sb("carry_rows", [1, 2 * P])
        carry = sb("carry", [1, HEADS, CHAINS + 1])
        ends = sb("ends", [1, 2], i32)
        flag = sb("flag", [1, 2], i32)
        LABEL = sb("LABEL", [P, NBP], i32)
        PS = ctx.enter_context(nc.psum_tensor("PS", [P, 8, GT * P], f32))

        S, F = HT[:, 0:SL], HT[:, SL:2 * SL]
        NEW = ACC[:, 0:SL + 1]
        KEEP = ACC[:, SL + 1:2 * SL + 2]
        assert 2 * SL + 2 <= NW + 4
        raw = G[:].bitcast(i32)
        assert TG * 2 <= RING * GT
        dst_raw, src_raw = raw[:, 0:TG, :], raw[:, TG:2 * TG, :]
        dst_f, src_f = EA[:, 0:TG, :], EA[:, TG:2 * TG, :]
        loc_f = MSG[:, 0:TG, :]
        next_raw, badly = H[:, 0:TG, :].bitcast(i32), H[:, TG:2 * TG, :]
        flat = lambda buf: buf[:].rearrange("p b f -> p (b f)")
        HITS, PROD = flat(X), flat(H)
        PLACE, NEWID, NODE = ACC[:, 0:NW], HT[:, 0:NW], DEG[:, 0:NW]
        lower = OH[:, 0, :]
        x_stage, pair, ea_stage = OH[:, 1, :], small[:, 0:2], EA[:, RING * GT - 1, :]
        sorted_in = flat(H)[:, 0:TG * P * 2].rearrange("p (g f two) -> p g f two", f=P, two=2)
        assert E % P > 1 and 2 * TG < RING * GT and 2 * TG <= NBP
        B01, B02, B11, B3, GAM, BET, E1, ATT = range(8)

        s_pre = sem("constants_ready")
        s_w = sem("weights_loaded")
        s_x = sem("x_loaded")
        s_raw = sem("edges_loaded")
        s_f = sem("edges_as_float")
        s_tp0 = sem("edges_transposed")
        s_ix = sem("edge_tables_ready")
        s_line = sem("dst_line_written")
        s_chain = sem("vector_step_done")
        s_achain = sem("scalar_step_done")
        s_x1 = sem("rows_updated")
        s_var = sem("variances_ready")
        s_rows = sem("outputs_added")
        s_deg0 = sem("degrees_cleared")
        s_rs = sem("deviations_inverted")
        s_sd = sem("deviations_ready")
        s_bsd = sem("batch_deviation_ready")
        s_bva = sem("batch_variance_ready")
        s_dsd = sem("degree_roots_ready")
        s_ln = sem("norm_scales_ready")
        s_h = sem("h_ready")
        s_tab = sem("table_written")
        s_tp = sem("h_transposed")
        s_acc0 = sem("accumulator_started")
        s_ht = sem("ht_ready")
        s_gath = [sem(f"gathered_{q}") for q in range(RING)]
        s_ea = [sem(f"edge_rows_loaded_{q}") for q in range(RING)]
        s_win = [sem(f"windows_loaded_{q}") for q in range(RING)]
        s_xj = [sem(f"xj_stored_{q}") for q in range(RING)]
        s_settle = sem("settled")
        s_idx = sem("indices_ready")
        s_msg = sem("messages_ready")
        s_relu = sem("messages_rectified")
        s_oh = sem("onehots_ready")
        s_mm = sem("group_products_done")
        s_add = sem("tile_added")
        s_m1 = sem("mlp_in_product")
        s_z = sem("mlp_hidden_ready")
        s_m2 = sem("row_product_done")
        s_yp = sem("layer1_output_product")
        s_y = sem("layer1_output_ready")
        s_dv = sem("sums_times_dinv")
        s_bn = sem("batch_norm_done")
        s_bns = sem("batch_norm_scales_ready")
        s_ohtp = sem("onehots_transposed")
        s_oht = sem("transposed_onehots_copied")
        s_zz = sem("edge_sums_ready")
        s_sl = sem("sloped_sums_ready")
        s_lk = sem("leaky_ready")
        s_lg = sem("logit_product_done")
        s_el = sem("logits_copied")
        s_lrp = sem("table_product_done")
        s_lrc = sem("table_rows_staged")
        s_lrt = [sem(f"staged_rows_written_{par}") for par in range(2)]
        s_sort = sem("logits_by_chain")
        s_sc = sem("scan_input_transposed")
        s_scc = sem("scan_input_copied")
        s_seg = sem("scan_lines_loaded")
        s_cr = sem("chain_ends_ready")
        s_crt = sem("chain_ends_transposed")
        s_ci = sem("carries_ready")
        s_cit = sem("carries_transposed")
        s_sub = sem("logits_shifted")
        s_exp = sem("exponentials_ready")
        s_al = sem("weights_ready")
        s_alt = sem("weights_transposed")
        s_alc = sem("weights_copied")
        s_az = sem("accumulator_cleared")
        s_out = sem("output_written")
        s_awp = sem("distances_spread")
        s_awd = sem("destinations_by_group")
        s_bad = sem("disorder_counted")
        s_badt = sem("disorder_transposed")
        s_flag = sem("flag_ready")
        s_sstep = sem("sort_vector_step_done")
        s_scon = sem("sort_constants_ready")
        s_sdst = sem("sort_destinations_transposed")
        s_shits = sem("sort_hits_summed")
        s_scnt = sem("sort_counts_product")
        s_scc2 = sem("sort_counts_copied")
        s_sxs = sem("sort_rows_staged")
        s_sxw = sem("sort_rows_scattered")
        s_soh = sem("sort_onehot_ready")
        s_sp = sem("sort_products_done")
        s_sq = sem("sort_products_used")
        s_sst = sem("sort_places_ready")
        s_sea = sem("sort_edge_rows_loaded")
        s_spw = sem("sort_pairs_scattered")
        s_sew = sem("sort_edge_rows_scattered")
        s_scl = sem("sort_buffers_cleared")
        s_sld = sem("sorted_inputs_loaded")
        s_sf = sem("sorted_edges_as_float")
        s_stp = sem("sorted_edges_transposed")
        s_sdone = sem("sorted_tables_ready")
        s_us = sem("unsort_rows_stored")
        s_ui = sem("unsort_indices_ready")
        s_ug = sem("unsort_rows_gathered")

        CREDIT = 4
        DMA_CREDIT = 16
        mm = lambda g: g + (CREDIT + 1)
        added = lambda g: g * GT + (GT * (CREDIT + 1))

        lr_stored = lambda par: 32 * (CHUNKS // 2 + 1 - par)
        g3_stored = lambda par: 48 * (CHUNKS // 2 + 1 - par)

        def settle(eng):
            eng.sem_inc(s_settle, 1)

        def window_starts(which, i, grouped):
            here = GWIN[0:1, bass.ds(i * RING, RING)] if grouped else WIN[0:1, bass.ds(i * (RING * GT), RING * GT)]
            return nc.values_load_multi_w_load_instructions(
                here, engines=[which], min_val=0, max_val=N,
                skip_runtime_bounds_check_because="a window starts at a destination, or at N in the padding")[1]

        def chunks(eng, body):
            with eng.Fori(0, CHUNKS // 2) as j:
                body(2 * j, 0)
                body(2 * j + 1, 1)
            body(CHUNKS - 1, 0)

        UNITS = CHUNKS // 2 + 1

        def blocks(buf, u, size):
            return buf[:, bass.ds(u * (2 * CB), size * CB)]

        def nodes(buf, c):
            return buf[:, bass.ds(c * CB, CB), :]

        def wide(buf, c):
            return buf[:, bass.ds(c * (CB * P), CB * P)]

        def disordered(eng):
            return eng.value_load(flag[0:1, 0:1], min_val=0, max_val=1)

        def either(eng, body):
            with eng.If(eng.value_load(flag[0:1, 1:2], min_val=0, max_val=1) != 0):
                body(False)
            with eng.Else():
                body(True)

        tail_slot = FULL - (ITERS - 1) * RING * GT

        def ea_before(q):
            return 16 * ITERS + (16 if q == tail_slot // GT else 0)

        A0, A1, AB, A3 = range(4)
        G0, G1, GA, G3 = range(4)

        block = ctx.enter_context(nc.Block())

        @block.sync
        def _(sp):
            def edges(view, ap, n):
                full = FULL // P
                last = FULL - full * P
                sp.dma_start(view[:, 0:full, :], ap[0:full * P * P].rearrange("(g p f) -> p g f", p=P, f=P)).then_inc(s_raw, 16)
                sp.dma_start(view[0:last, full, :], ap[full * P * P:FULL * P].rearrange("(p f) -> p f", f=P)).then_inc(s_raw, 16)
                sp.dma_start(view[last:last + 1, full, 0:n - FULL * P], ap[FULL * P:n].unsqueeze(0)).then_inc(s_raw, 16)

            sp.wait_ge(s_pre, 1)
            edges(dst_raw, dst, E)
            edges(src_raw, src, E)
            edges(next_raw, dst[1:E], E - 1)
            sp.dma_start(X[:, 0:NB - 1, :], x[0:(NB - 1) * P, :].rearrange("(b p) f -> p b f", p=P)).then_inc(s_x, 16)
            sp.dma_start(X[0:REST, NB - 1, :], x[(NB - 1) * P:N, :]).then_inc(s_x, 16)
            for name, ap in (("g0_1", g0_w1), ("g0_2", g0_w2), ("g1_1", g1_w1), ("g1_2", g1_w2), ("g3", g3_w), ("ln_raw", g3_wln)):
                sp.dma_start(W[name][:], ap).then_inc(s_w, 16)
            sp.dma_start(WLR[:, 0:P], g2_wl).then_inc(s_w, 16)
            sp.dma_start(WLR[:, P:2 * P], g2_wr).then_inc(s_w, 16)
            for c, ap in ((B01, g0_b1), (B02, g1_b2), (B11, g1_b1), (B3, g3_b), (GAM, g1_gamma), (BET, g1_beta)):
                sp.dma_start(cols[:, c:c + 1], ap.unsqueeze(1)).then_inc(s_w, 16)
            sp.dma_start(cols[:, ATT:ATT + 1], g2_att.rearrange("a h f -> (h f) a")).then_inc(s_w, 16)
            sp.dma_start(cols[:, E1:E1 + 1], g0_eps.unsqueeze(0).to_broadcast([P, 1])).then_inc(s_w, 16)
            for c, ap in ((0, g0_b2), (1, g2_bias)):
                sp.dma_start(rows[:, c, :], ap.unsqueeze(0).to_broadcast([P, P])).then_inc(s_w, 16)

            def by_tile(view, ap):
                whole = T // P
                return ((view[:, 0:whole], ap[0:whole * P * P].rearrange("(g p f) -> p g f", p=P, f=P)),
                        (view[0:T - whole * P, whole], ap[whole * P * P:T * P].rearrange("(p f) -> p f", f=P)))

            sp.wait_ge(s_flag, 1)
            with sp.If(disordered(sp) != 0):
                sp.wait_ge(s_sxs, 1)
                with sp.Fori(0, FULL) as t:
                    sp.wait_ge(s_sew, t * 16 + DMA_CREDIT)
                    sp.dma_start(ea_stage, edge_attr[bass.ds(t * P, P), :]).then_inc(s_sea, 16)
                sp.wait_ge(s_sew, FULL * 16 + DMA_CREDIT)
                sp.dma_start(ea_stage[0:E - FULL * P, :], edge_attr[FULL * P:E, :]).then_inc(s_sea, 16)
                sp.wait_ge(s_scl, 1)
                sp.wait_ge(s_spw, T * 16 + DMA_CREDIT)
                sp.wait_ge(s_sew, (FULL + 1) * 16 + DMA_CREDIT)
                sp.wait_ge(s_sxw, NBP * 16 + DMA_CREDIT)
                sp.dma_start(X[:], sorted_x.rearrange("(b p) f -> p b f", p=P)).then_inc(s_sld, 16)
                whole = T // P
                sp.dma_start(sorted_in[:, 0:whole].rearrange("p g f two -> p g (f two)"),
                             sorted_pairs[0:whole * P * P, :].rearrange("(g p f) two -> p g (f two)", p=P, f=P)).then_inc(s_sld, 16)
                sp.dma_start(sorted_in[0:T - whole * P, whole].rearrange("p f two -> p (f two)"),
                             sorted_pairs[whole * P * P:T * P, :].rearrange("(p f) two -> p (f two)", f=P)).then_inc(s_sld, 16)
                sp.wait_ge(s_sdone, 1)

            for here, there in by_tile(dst_raw, dst_line[1:T * P + 1]):
                sp.dma_start(there, here).then_inc(s_line, 16)
            sp.dma_start(dst_line[0:1].unsqueeze(0), ends[:, 0:1]).then_inc(s_line, 16)
            sp.dma_start(dst_line[T * P + 1:T * P + 2].unsqueeze(0), ends[:, 1:2]).then_inc(s_line, 16)

            def store_table(n, count):
                view = table[n].rearrange("(b p) f -> p b f", p=P)

                def one(c, _):
                    sp.wait_ge(s_h, c + (CHUNKS * count + 1))
                    sp.dma_start(view[:, bass.ds(c * CB, CB), :], nodes(H, c)).then_inc(s_tab, 16)
                chunks(sp, one)

            store_table(0, 0)

            def load_layer0(rows_of_edges):
                ea_view = rows_of_edges[0:FULL * P, :].rearrange("(t p) f -> p t f", p=P)

                def load_ea(i, q, tiles=GT):
                    sp.wait_ge(s_msg, i * RING + (q + 1))
                    sp.dma_start(EA[:, q * GT:q * GT + tiles, :], ea_view[:, bass.ds(i * (RING * GT) + q * GT, tiles), :]).then_inc(s_ea[q], 16)
                with sp.Fori(0, ITERS - 1) as i:
                    for q in range(RING):
                        load_ea(i, q)
                for q in range(RING):
                    here = min(GT, FULL - ((ITERS - 1) * RING + q) * GT)
                    assert here > 0
                    load_ea(ITERS - 1, q, here)
                sp.dma_start(EA[0:E - FULL * P, tail_slot, :], rows_of_edges[FULL * P:E, :]).then_inc(s_ea[tail_slot // GT], 16)
            with sp.If(disordered(sp) != 0):
                load_layer0(sorted_ea)
            with sp.Else():
                load_layer0(edge_attr)

            store_table(1, 1)

            sp.wait_ge(s_line, 16 * 4)
            sp.wait_ge(s_m2, 2 * CHUNKS)
            for off, where in ((1, NEW), (0, KEEP)):
                line = bass.AP(dst_line.tensor, off, [[SL, CHAINS], [1, SL + 1]])
                for h in range(HEADS):
                    sp.dma_start(where[h * CHAINS:(h + 1) * CHAINS, :].bitcast(i32), line).then_inc(s_seg, 16)

            hl_view = hl_table.rearrange("(b p) f -> p b f", p=P)
            hr_view = table[2].rearrange("(b p) f -> p b f", p=P)

            def store_lr(c, par):
                sp.wait_ge(s_lrc, c + 1)
                sp.dma_start(hl_view[:, bass.ds(c * CB, CB), :], EA[:, par * CB:(par + 1) * CB, :]).then_inc(s_lrt[par], 16)
                sp.dma_start(hr_view[:, bass.ds(c * CB, CB), :], G[:, par * CB:(par + 1) * CB, :]).then_inc(s_lrt[par], 16)
            chunks(sp, store_lr)
            for par in range(2):
                sp.wait_ge(s_lrt[par], lr_stored(par))

            def load_windows(starts, q, grouped):
                for k in range(1 if grouped else GT):
                    sp.dma_start(EA[:, q * GT + k, :], hl_table[bass.ds(starts[q if grouped else q * GT + k], P), :]).then_inc(s_win[q], 16)

            def keep_xj(i, q):
                sp.wait_ge(s_gath[q], i * (16 * GT) + 16 * GT * (GA * ITERS + 1))
                sp.dma_start(xj_store[bass.ds(i * RING + q, 1), :, :].rearrange("a p f -> p (a f)"),
                             G[:, q * GT:(q + 1) * GT, :].rearrange("p k f -> p (k f)")).then_inc(s_xj[q], 16)

            def attention_loads(grouped):
                starts = window_starts(mybir.EngineType.SP, 0, grouped)
                for q in range(RING):
                    load_windows(starts, q, grouped)
                with sp.Fori(0, ITERS - 1) as i:
                    starts = window_starts(mybir.EngineType.SP, i + 1, grouped)
                    for q in range(RING):
                        keep_xj(i, q)
                        sp.wait_ge(s_zz, i * RING + (q + 1))
                        load_windows(starts, q, grouped)
                for q in range(RING):
                    keep_xj(ITERS - 1, q)
            either(sp, attention_loads)

            sp.wait_ge(s_zz, GROUPS)
            def load_xj(i, q):
                sp.wait_ge(s_msg, i * RING + (GROUPS + q + 1))
                sp.dma_start(EA[:, q * GT:(q + 1) * GT, :].rearrange("p k f -> p (k f)"),
                             xj_store[bass.ds(i * RING + q, 1), :, :].rearrange("a p f -> p (a f)")).then_inc(s_ea[q], 16)
            for q in range(RING):
                sp.wait_ge(s_xj[q], 16 * ITERS + DMA_CREDIT)
            with sp.Fori(0, ITERS) as i:
                for q in range(RING):
                    load_xj(i, q)

            g3_view = table[3].rearrange("(b p) f -> p b f", p=P)

            def store_g3(c, par):
                sp.wait_ge(s_lrc, c + (CHUNKS + 1))
                sp.dma_start(g3_view[:, bass.ds(c * CB, CB), :], G[:, par * CB:(par + 1) * CB, :]).then_inc(s_lrt[par], 16)
            chunks(sp, store_g3)

            with sp.If(disordered(sp) != 0):
                sp.wait_ge(s_x1, CHUNKS)
                sp.dma_start(sorted_x.rearrange("(b p) f -> p b f", p=P), X[:]).then_inc(s_us, 16)

                def put_back(b, n):
                    sp.wait_ge(s_ug, b * 16 + (16 + DMA_CREDIT))
                    sp.dma_start(out[bass.ds(b * P, n), :], G[0:n, 0, :]).then_inc(s_out, 16)
                with sp.Fori(0, NB - 1) as b:
                    put_back(b, P)
                put_back(NB - 1, REST)
                sp.wait_ge(s_out, NB * 16 + DMA_CREDIT)
            with sp.Else():
                whole = (NB - 1) // CB
                out_view = out[0:(NB - 1) * P, :].rearrange("(b p) f -> p b f", p=P)
                with sp.Fori(0, whole) as c:
                    sp.wait_ge(s_x1, c + 1)
                    sp.dma_start(out_view[:, bass.ds(c * CB, CB), :], nodes(X, c)).then_inc(s_out, 16)
                sp.wait_ge(s_x1, CHUNKS)
                if whole * CB < NB - 1:
                    sp.dma_start(out_view[:, whole * CB:NB - 1, :], X[:, whole * CB:NB - 1, :]).then_inc(s_out, 16)
                sp.dma_start(out[(NB - 1) * P:N, :], X[0:REST, NB - 1, :]).then_inc(s_out, 16)
                sp.wait_ge(s_out, 16 * (whole + (whole * CB < NB - 1) + 1) + DMA_CREDIT)

        @block.gpsimd
        def _(pool):
            nc.gpsimd.memset(dst_raw, N)
            nc.gpsimd.memset(src_raw, 0)
            nc.gpsimd.memset(next_raw, N)
            nc.gpsimd.memset(ends[:, 0:1], -1)
            nc.gpsimd.memset(ends[:, 1:2], N + 1)
            nc.gpsimd.memset(X[:, NB - 1:NBP, :], 0.0).then_inc(s_pre, 1)
            nc.gpsimd.memset(ones[:], 1.0)
            nc.gpsimd.memset(consts[:, 0:1], LN_EPS)
            nc.gpsimd.memset(consts[:, 1:2], 1.0)
            nc.gpsimd.memset(att4[:], 0.0)
            nc.gpsimd.iota(iota_row[:], [[1, P]], base=0, channel_multiplier=0, allow_small_or_imprecise_dtypes=True)
            nc.gpsimd.memset(ident[:], 0.0).then_inc(s_pre, 1)
            pool.wait_ge(s_pre, 2)
            nc.gpsimd.affine_select(out=ident[:], in_=ident[:], compare_op=ALU.not_equal, fill=1.0, base=0,
                                    pattern=[[-1, P]], channel_multiplier=1).then_inc(s_pre, 1)
            nc.gpsimd.memset(DEG, 0.0).then_inc(s_deg0, 1)

            pool.wait_ge(s_flag, 1)
            with pool.If(disordered(pool) != 0):
                pool.wait_ge(s_deg0, 1)
                nc.gpsimd.iota(NODE, [[1, NW]], base=0, channel_multiplier=0, allow_small_or_imprecise_dtypes=True)
                nc.gpsimd.affine_select(out=lower, in_=ones[:], compare_op=ALU.is_gt, fill=0.0, base=0,
                                        pattern=[[1, P]], channel_multiplier=-1).then_inc(s_scon, 1)
                with pool.Fori(0, NBP) as b:
                    pool.wait_ge(s_sxs, b + 1)
                    settle(pool)
                    nc.gpsimd.indirect_dma_start(sorted_x, bass.IndirectOffsetOnAxis(IDX[:, 0:1], 0), x_stage, None).then_inc(s_sxw, 16)

                def place_pairs(t):
                    pool.wait_ge(s_sst, t + 1)
                    settle(pool)
                    nc.gpsimd.indirect_dma_start(sorted_pairs, bass.IndirectOffsetOnAxis(IDX[:, 0:1], 0), pair, None).then_inc(s_spw, 16)

                def place_rows(t):
                    pool.wait_ge(s_sea, t * 16 + 16)
                    settle(pool)
                    nc.gpsimd.indirect_dma_start(sorted_ea, bass.IndirectOffsetOnAxis(IDX[:, 0:1], 0), ea_stage, None).then_inc(s_sew, 16)
                with pool.Fori(0, FULL + 1) as t:
                    pool.wait_ge(s_sst, t + 1)
                    place_rows(t)
                    pool.wait_ge(s_sew, t * 16 + (16 + DMA_CREDIT))
                    place_pairs(t)
                for t in range(FULL + 1, T):
                    place_pairs(t)
                pool.wait_ge(s_spw, T * 16 + DMA_CREDIT)

            def gather(n, before, ready):
                for s, value in ready:
                    pool.wait_ge(s, value)
                with pool.Fori(0, ITERS) as i:
                    for q in range(RING):
                        before(i, q)
                        pool.wait_ge(s_idx, i * RING + (n * GROUPS + q + 1))
                        settle(pool)
                        for k in range(GT):
                            slot = q * GT + k
                            nc.gpsimd.indirect_dma_start(
                                G[:, slot, :], None, table[n],
                                bass.IndirectOffsetOnAxis(IDX[:, slot:slot + 1], 0)).then_inc(s_gath[q], 16)

            gather(G0, lambda i, q: pool.wait_ge(s_msg, i * RING + (q + 1)), [(s_tab, 16 * CHUNKS)])
            gather(G1, lambda i, q: pool.wait_ge(s_mm, mm(i * RING + (q - RING + A1 * GROUPS))), [(s_tab, 32 * CHUNKS)])

            def attention_slot(i, q):
                pool.wait_ge(s_xj[q], i * 16 + DMA_CREDIT)
                pool.wait_ge(s_el, i * RING + (q + 1))
            gather(GA, attention_slot, [(s_lrt[par], lr_stored(par)) for par in range(2)])

            pool.wait_ge(s_al, 1)
            nc.gpsimd.memset(ACC, 0.0).then_inc(s_az, 1)
            for q in range(RING):
                pool.wait_ge(s_xj[q], 16 * ITERS + DMA_CREDIT)
            pool.wait_ge(s_alc, -(-SEG // GT))
            with pool.Fori(0, ITERS) as i:
                for q in range(RING):
                    pool.wait_ge(s_mm, mm(i * RING + (q - RING + AB * GROUPS)))
                    pool.wait_ge(s_ea[q], i * 16 + (ea_before(q) + 16))
                    weight = EL[:, bass.ds(i * (RING * GT) + q * GT, GT), :].rearrange("p k h -> p (k h)").unsqueeze(2).to_broadcast([P, GT * HEADS, HF])
                    nc.gpsimd.tensor_tensor(G[:, q * GT:(q + 1) * GT, :].rearrange("p k (h f) -> p (k h) f", h=HEADS),
                                            EA[:, q * GT:(q + 1) * GT, :].rearrange("p k (h f) -> p (k h) f", h=HEADS),
                                            weight, ALU.mult).then_inc(s_msg, 1)

            gather(G3, lambda i, q: pool.wait_ge(s_mm, mm(i * RING + (q - RING + A3 * GROUPS))), [(s_lrt[par], g3_stored(par)) for par in range(2)])
            with pool.If(disordered(pool) != 0):
                pool.wait_ge(s_us, 16)
                with pool.Fori(0, NB) as b:
                    pool.wait_ge(s_ui, b + 1)
                    pool.wait_ge(s_out, b * 16 + DMA_CREDIT)
                    settle(pool)
                    nc.gpsimd.indirect_dma_start(G[:, 0, :], None, sorted_x, bass.IndirectOffsetOnAxis(IDX[:, 0:1], 0)).then_inc(s_ug, 16)
                pool.wait_ge(s_ug, NB * 16 + DMA_CREDIT)

        @block.scalar
        def _(act):
            chain = Chain(act, s_achain)
            act.sem_inc(s_el, CREDIT)

            def indices(n, i, q):
                act.wait_ge(s_gath[q], i * (16 * GT) + 16 * GT * n * ITERS)
                nc.scalar.copy(IDX[:, q * GT:(q + 1) * GT], SRC[:, bass.ds(i * (RING * GT) + q * GT, GT)]).then_inc(s_idx, 1)

            def turns(n, body, peel=0):
                for q in range(RING):
                    indices(n, 0, q)
                for i in range(peel):
                    for q in range(RING):
                        body(i, q)
                        indices(n, i + 1, q)
                with act.Fori(peel, ITERS - 1) as i:
                    for q in range(RING):
                        body(i, q)
                        indices(n, i + 1, q)
                for q in range(RING):
                    body(ITERS - 1, q)

            def norm_rows(n, before=lambda c, par: None):
                def prepare(u, size):
                    for par in range(size):
                        before(2 * u + par, par)

                def deviations(u, size):
                    act.wait_ge(s_var, u + (n * UNITS + 1))
                    nc.scalar.activation(blocks(SD, u, size), MVS[:, bass.ds(u * (2 * CB), size * CB), 1], ACT.Sqrt,
                                         bias=consts[:, 0:1]).then_inc(s_sd, 1)

                def rows_of(u, size):
                    act.wait_ge(s_ln, u + (n * UNITS + 1))
                    for k in range(size * CB):
                        at = u * (2 * CB) + k
                        last = nc.scalar.activation(
                            H[:, bass.ds(at, 1), :].rearrange("p a f -> p (a f)"),
                            X[:, bass.ds(at, 1), :].rearrange("p a f -> p (a f)"),
                            ACT.Relu, bias=NM[:, bass.ds(at, 1)], scale=RS[:, bass.ds(at, 1)])
                        if k % CB == CB - 1:
                            last.then_inc(s_h, 1)
                prepare(0, 2)
                prepare(1, 2)
                deviations(0, 2)
                if n:
                    act.wait_ge(s_tab, 16 * CHUNKS * min(n, 2))
                with act.Fori(1, UNITS - 2) as u:
                    prepare(u + 1, 2)
                    deviations(u, 2)
                    rows_of(u - 1, 2)
                prepare(UNITS - 1, 1)
                deviations(UNITS - 2, 2)
                rows_of(UNITS - 3, 2)
                deviations(UNITS - 1, 1)
                rows_of(UNITS - 2, 2)
                rows_of(UNITS - 1, 1)

            def copy_transposed(n, to, what):
                def one(c, par):
                    act.wait_ge(s_tp, c + (n * CHUNKS + 1))
                    nc.scalar.copy(wide(to, c), PS[:, par, :]).then_inc(what, 1)
                chunks(act, one)

            def hidden_chunk(n, bias, c, par):
                act.wait_ge(s_m1, c + (n * CHUNKS + 1))
                nc.scalar.activation(MSG[:, par * GT:(par + 1) * GT, :].rearrange("p k f -> p (k f)"), PS[:, 4 + par, :],
                                     ACT.Relu, bias=cols[:, bias:bias + 1]).then_inc(s_z, 1)

            act.wait_ge(s_pre, 3)
            norm_rows(0)
            act.wait_ge(s_ix, 2)

            def rectify(i, q):
                act.wait_ge(s_msg, i * RING + (CREDIT + q + 1))
                m = MSG[:, (q % 2) * GT:(q % 2 + 1) * GT, :]
                nc.scalar.activation(m, m, ACT.Relu).then_inc(s_relu, 1)
            turns(G0, rectify)
            norm_rows(1, lambda c, par: hidden_chunk(0, B01, c, par))
            copy_transposed(1, ACC, s_acc0)
            turns(G1, lambda i, q: None)
            def output1(c, par):
                act.wait_ge(s_yp, c + 1)
                nc.scalar.activation(wide(ACC, c), PS[:, 6 + par, :], ACT.Identity, bias=cols[:, B02:B02 + 1]).then_inc(s_y, 1)
            hidden_chunk(1, B11, 0, 0)
            with act.Fori(0, CHUNKS // 2) as j:
                for par in range(2):
                    hidden_chunk(1, B11, 2 * j + (par + 1), 1 - par)
                    output1(2 * j + par, par)
            output1(CHUNKS - 1, 0)
            act.wait_ge(s_bva, 1)
            nc.scalar.activation(small[:, 4:5], small[:, 4:5], ACT.Sqrt).then_inc(s_bsd, 1)
            act.wait_ge(s_bns, 1)

            def batch_norm(c, _):
                nc.scalar.activation(wide(ACC, c), wide(ACC, c), ACT.Identity, bias=small[:, 3:4], scale=small[:, 2:3]).then_inc(s_bn, 1)
            norm_rows(2, batch_norm)
            copy_transposed(2, HT, s_ht)

            def stage_lr(c, par):
                act.wait_ge(s_lrp, c + 1)
                nc.scalar.copy(EA[:, par * CB:(par + 1) * CB, :].rearrange("p (b s) f -> p b s f", s=2),
                               PS[:, 4 + 2 * par:6 + 2 * par, :].rearrange("p b (s w f) -> p b w s f", s=2, w=2)[:, :, 0])
                nc.scalar.copy(G[:, par * CB:(par + 1) * CB, :].rearrange("p (b s) f -> p b s f", s=2),
                               PS[:, 4 + 2 * par:6 + 2 * par, :].rearrange("p b (s w f) -> p b w s f", s=2, w=2)[:, :, 1]).then_inc(s_lrc, 1)

            stage_lr(0, 0)
            stage_lr(1, 1)
            with act.Fori(1, CHUNKS // 2) as j:
                for par in range(2):
                    act.wait_ge(s_lrt[par], j * 32)
                    stage_lr(2 * j + par, par)
            act.wait_ge(s_lrt[0], CHUNKS // 2 * 32)
            stage_lr(CHUNKS - 1, 0)
            nc.scalar.activation(DEG, DEG, ACT.Sqrt, bias=consts[:, 1:2]).then_inc(s_dsd, 1)

            def copy_oht(i, q):
                b = q % 2
                act.wait_ge(s_ohtp, i * RING + (q + 1))
                nc.scalar.copy(OHT[:, b * GT:(b + 1) * GT, :].rearrange("p k f -> p (k f)"), PS[:, b, :]).then_inc(s_oht, 1)

            def copy_logits(i, q):
                b = q % 2
                act.wait_ge(s_lg, i * RING + (q + 1))
                nc.scalar.copy(EL[:, bass.ds(i * (RING * GT) + q * GT, GT), :],
                               PS[:, 4 + b, 0:GT * HEADS].rearrange("p (k h) -> p k h", h=HEADS)).then_inc(s_el, 1)

            def attend(i, q):
                if q < RING - 1:
                    copy_oht(i, q + 1)
                elif not isinstance(i, int) or i < ITERS - 1:
                    copy_oht(i + 1, 0)
                b = q % 2
                act.wait_ge(s_zz, i * RING + (q + 1))
                nc.scalar.mul(MSG[:, b * GT:(b + 1) * GT, :].rearrange("p k f -> p (k f)"), PS[:, 2 + b, :], SLOPE).then_inc(s_sl, 1)
                if q > 0:
                    copy_logits(i, q - 1)
                elif not isinstance(i, int) or i > 0:
                    copy_logits(i - 1, RING - 1)
            copy_oht(0, 0)
            turns(GA, attend, 1)
            copy_logits(ITERS - 1, RING - 1)

            for n, g in enumerate(range(0, SEG, GT)):
                w = min(GT, SEG - g)
                act.wait_ge(s_sc, n + 1)
                nc.scalar.copy(S[:, g * P:(g + w) * P], PS[:, n % 2, 0:w * P]).then_inc(s_scc, 1)
            act.wait_ge(s_sub, 1)
            nc.scalar.activation(S, S, ACT.Exp).then_inc(s_exp, 1)

            norm_rows(3)
            def stage_g3(c, par):
                nc.scalar.copy(G[:, par * CB:(par + 1) * CB, :].rearrange("p k f -> p (k f)"), PS[:, 4 + par, :]).then_inc(s_lrc, 1)
                nc.scalar.copy(wide(ACC, c), PS[:, 6 + par, :]).then_inc(s_ht, 1)
            for c in (0, 1):
                act.wait_ge(s_lrp, CHUNKS + c + 1)
                stage_g3(c, c)
            with act.Fori(1, CHUNKS // 2) as j:
                for par in range(2):
                    act.wait_ge(s_lrt[par], j * 16 + lr_stored(par))
                    act.wait_ge(s_lrp, j * 2 + (par + CHUNKS + 1))
                    stage_g3(2 * j + par, par)
            act.wait_ge(s_lrt[0], CHUNKS // 2 * 16 + lr_stored(0))
            act.wait_ge(s_lrp, 2 * CHUNKS)
            stage_g3(CHUNKS - 1, 0)
            turns(G3, lambda i, q: None)

            def hidden3(c, par):
                act.wait_ge(s_dv, c + 1)
                nc.scalar.activation(MSG[:, par * GT:(par + 1) * GT, :], MSG[:, par * GT:(par + 1) * GT, :],
                                     ACT.Relu, bias=cols[:, B3:B3 + 1]).then_inc(s_z, 1)
            chunks(act, hidden3)

        @block.vector
        def _(dve):
            chain = Chain(dve, s_chain)
            dve.sem_inc(s_msg, CREDIT)
            dve.sem_inc(s_add, GT * CREDIT)
            for free in s_xj + [s_sew, s_sxw, s_spw, s_ug, s_out]:
                dve.sem_inc(free, DMA_CREDIT)

            def relative():
                return nc.vector.tensor_tensor(loc_f, dst_f, dst_f[:, :, 0:1].to_broadcast([P, TG, P]), ALU.subtract)

            def edge_tables():
                nc.vector.tensor_copy(SRC[:], PS[:, 0:2, :].rearrange("p b f -> p (b f)")[:, 0:T])
                nc.vector.tensor_copy(LD[:], PS[:, 2:4, :].rearrange("p b f -> p (b f)")[:, 0:T])
                return nc.vector.tensor_copy(WIN[:], PS[0:1, 4:6, :].rearrange("p b f -> p (b f)")[:, 0:T])

            dve.wait_ge(s_raw, 16 * 9)
            nc.vector.tensor_copy(src_f, src_raw)
            chain.one(nc.vector.tensor_copy(dst_f, dst_raw))
            relative().then_inc(s_f, 1)
            chain.one(nc.vector.tensor_tensor(badly, dst_raw, next_raw, ALU.is_gt))
            dve.wait_ge(s_f, 1)
            chain.one(nc.vector.scalar_tensor_tensor(badly, loc_f, P - 0.5, badly, ALU.is_gt, ALU.max))
            nc.vector.tensor_reduce(small[:, 6:7], badly.rearrange("p g f -> p (g f)"), AX.X, ALU.max).then_inc(s_bad, 1)
            dve.wait_ge(s_tp0, 1)
            edge_tables().then_inc(s_ix, 1)
            dve.wait_ge(s_badt, 1)
            chain.one(nc.vector.tensor_reduce(small[0:1, 0:1], PS[0:1, 7, 0:P], AX.X, ALU.max))
            starts_by_group = WIN[:].rearrange("a (g k) -> a g k", k=GT)
            dve.wait_ge(s_ix, 1)
            chain.one(nc.vector.tensor_copy(GWIN[:], starts_by_group[:, :, 0]))
            nc.vector.tensor_tensor(away[:].rearrange("a (g k) -> a g k", k=GT), starts_by_group,
                                    starts_by_group[:, :, 0:1].to_broadcast([1, GROUPS, GT]), ALU.subtract)
            nc.vector.memset(spread[:, GROUPS - 1:GROUPS], N)
            chain.one(nc.vector.tensor_copy(spread[:, 0:GROUPS - 1], GWIN[:, 1:GROUPS]))
            chain.one(nc.vector.tensor_tensor(spread[:], spread[:], GWIN[:], ALU.subtract))
            chain.one(nc.vector.tensor_reduce(small[0:1, 1:2], spread[:], AX.X, ALU.max))
            chain.one(nc.vector.tensor_scalar(small[0:1, 1:2], small[0:1, 1:2], P - 0.5, None, ALU.is_gt))
            chain.one(nc.vector.tensor_tensor(small[0:1, 1:2], small[0:1, 0:1], small[0:1, 1:2], ALU.max))
            nc.vector.tensor_copy(flag[:], small[0:1, 0:2]).then_inc(s_flag, 1)

            dve.wait_ge(s_flag, 1)
            with dve.If(disordered(dve) != 0):
                step = Chain(dve, s_sstep)
                dve.sem_inc(s_sq, 2)
                dve.wait_ge(s_x, 32)
                dve.wait_ge(s_scon, 1)
                dve.wait_ge(s_sdst, 1)
                nc.vector.tensor_copy(LD[:], PS[:, 4:6, :].rearrange("p b f -> p (b f)")[:, 0:T])
                step.one(nc.vector.memset(PLACE, 0.0))

                def hits(to, which, t):
                    return nc.vector.tensor_tensor(to, NODE, which[:, bass.ds(t, 1)].to_broadcast([P, NW]), ALU.is_equal)

                def chosen(to, values, at):
                    step.link(nc.vector.tensor_tensor(PROD, values, HITS, ALU.mult))
                    step.link(nc.vector.tensor_reduce(to, PROD, AX.X, ALU.add))

                with dve.Fori(0, T) as t:
                    step.at(t, 2)
                    step.link(hits(PROD, LD, t))
                    step.link(nc.vector.tensor_tensor(PLACE, PLACE, PROD, ALU.add))
                step.done(T, 2)
                nc.vector.memset(small[:, 6:7], 0.0).then_inc(s_shits, 1)
                for c in range(CHUNKS):
                    dve.wait_ge(s_scnt, c + 1)
                    nc.vector.tensor_copy(NEWID[:, c * CB * P:(c + 1) * CB * P], PS[:, c % 2, :]).then_inc(s_scc2, 1)
                dve.wait_ge(s_scc2, CHUNKS)
                every = ones[:, 0:1].to_broadcast([P, NW])
                step.one(nc.vector.tensor_scalar(PROD, NEWID, 0.5, None, ALU.is_gt))
                step.one(nc.vector.tensor_tensor_scan(PLACE, every, NEWID, 0.0, ALU.mult, ALU.add))
                step.one(nc.vector.tensor_tensor(PLACE, PLACE, NEWID, ALU.subtract))
                step.one(nc.vector.tensor_tensor_scan(NEWID, every, PROD, 0.0, ALU.mult, ALU.add))
                step.one(nc.vector.tensor_copy(small[:, 0:1], NEWID[:, N - 1:N]))
                step.one(nc.vector.tensor_scalar(small[:, 1:2], small[:, 0:1], -1.0, -1.0, ALU.mult, ALU.add))
                step.one(nc.vector.tensor_tensor(NEWID, NODE, NEWID, ALU.subtract))
                step.one(nc.vector.scalar_tensor_tensor(NODE, NEWID, -2.0, NODE, ALU.mult, ALU.add))
                step.one(nc.vector.scalar_tensor_tensor(PROD, NODE, small[:, 1:2], PROD, ALU.add, ALU.mult))
                step.one(nc.vector.scalar_tensor_tensor(NODE, NEWID, 2.0, NODE, ALU.mult, ALU.add))
                step.one(nc.vector.scalar_tensor_tensor(NEWID, NEWID, small[:, 0:1], PROD, ALU.add, ALU.add))
                step.one(nc.vector.tensor_copy(NEWID[:, N:NW], NODE[:, N:NW]))
                step.one(nc.vector.tensor_tensor(H[:], NEWID.rearrange("p (b f) -> p b f", f=P),
                                                 ident[:].unsqueeze(1).to_broadcast([P, NBP, P]), ALU.mult))
                step.one(nc.vector.tensor_reduce(SD[:], H[:], AX.X, ALU.add))
                step.one(nc.vector.tensor_copy(LABEL[:], SD[:]))
                with dve.Fori(0, NBP) as b:
                    dve.wait_ge(s_sxw, b * 16 + DMA_CREDIT)
                    nc.vector.tensor_copy(IDX[:, 0:1], LABEL[:, bass.ds(b, 1)])
                    nc.vector.tensor_copy(x_stage.unsqueeze(1), X[:, bass.ds(b, 1), :]).then_inc(s_sxs, 1)
                dve.wait_ge(s_sxw, NBP * 16 + DMA_CREDIT)
                with dve.Fori(0, T) as t:
                    step.at(t, 8)
                    hits(HITS, LD, t).then_inc(s_soh, 1)
                    for c in range(CHUNKS):
                        cols_c = slice(c * CB * P, (c + 1) * CB * P)
                        dve.wait_ge(s_sp, t * CHUNKS + (c + 1))
                        nc.vector.tensor_tensor(PROD[:, cols_c], PLACE[:, cols_c], PS[:, 2 * (c % 2), :], ALU.add)
                        nc.vector.tensor_tensor(PLACE[:, cols_c], PLACE[:, cols_c], PS[:, 2 * (c % 2) + 1, :], ALU.add).then_inc(s_sq, 1)
                    dve.wait_ge(s_sq, t * CHUNKS + (CHUNKS + 2))
                    step.link(nc.vector.tensor_tensor(PROD, PROD, HITS, ALU.mult))
                    step.link(nc.vector.tensor_reduce(small[:, 2:3], PROD, AX.X, ALU.add))
                    dve.wait_ge(s_spw, t * 16 + DMA_CREDIT)
                    chosen(pair[:, 1:2], NEWID, t)
                    step.link(hits(HITS, SRC, t))
                    chosen(pair[:, 0:1], NEWID, t)
                    step.link(nc.vector.tensor_copy(IDX[:, 0:1], small[:, 2:3]))
                    nc.vector.memset(small[:, 3:4], 0.0).then_inc(s_sst, 1)
                step.done(T, 8)
                nc.vector.memset(DEG, 0.0)
                nc.vector.memset(H[:], 0.0)
                step.one(nc.vector.memset(X[:], 0.0))
                nc.vector.memset(small[:, 3:4], 0.0).then_inc(s_scl, 1)
                dve.wait_ge(s_sld, 16 * 3)
                nc.vector.tensor_copy(src_f, sorted_in[:, :, :, 0])
                nc.vector.tensor_copy(dst_raw, sorted_in[:, :, :, 1])
                step.one(nc.vector.tensor_copy(dst_f, sorted_in[:, :, :, 1]))
                relative().then_inc(s_sf, 1)
                dve.wait_ge(s_stp, 1)
                step.one(edge_tables())
                nc.vector.memset(small[:, 3:4], 0.0).then_inc(s_sdone, 1)

            def group_windows(grouped):
                if grouped:
                    dve.wait_ge(s_awp, 1)
                    nc.vector.tensor_tensor(LD[:], LD[:], PS[:, 4:6, :].rearrange("p b f -> p (b f)")[:, 0:T], ALU.add).then_inc(s_awd, 1)
                    dve.wait_ge(s_awd, 1)
                else:
                    dve.sem_inc(s_awd, 1)
            either(dve, group_windows)

            dve.wait_ge(s_w, 16 * 18)
            dve.wait_ge(s_pre, 3)
            chain.one(nc.vector.tensor_scalar(cols[:, E1:E1 + 1], cols[:, E1:E1 + 1], 1.0, None, ALU.add))
            for h in range(HEADS):
                last = nc.vector.tensor_copy(att4[h * HF:(h + 1) * HF, h:h + 1], cols[h * HF:(h + 1) * HF, ATT:ATT + 1])
            chain.one(last)
            dve.wait_ge(s_tp0, 2)
            chain.one(nc.vector.tensor_copy(W["ln"][:], PS[:, 6, 0:P]))
            nc.vector.memset(small[:, 7:8], 0.0).then_inc(s_ix, 1)

            def norm(n, layer=None):
                bank = 4 if layer == 1 else 6

                def statistics(u, size):
                    chain.at(u, 2)
                    if layer is not None:
                        for par in range(size):
                            dve.wait_ge(s_m2, 2 * u + (par + layer * CHUNKS + 1))
                            xc = nodes(X, 2 * u + par).rearrange("p b f -> p (b f)")
                            nc.vector.tensor_tensor(xc, xc, PS[:, bank + par, :], ALU.add).then_inc(s_rows, 1)
                        dve.wait_ge(s_rows, 2 * u + (size + layer * CHUNKS))
                    settle(dve)
                    for k in range(size * CB):
                        last = nc.vector.bn_stats(ST[:, k, :], X[:, bass.ds(u * (2 * CB) + k, 1), :].rearrange("p a f -> p (a f)"))
                    chain.link(last)
                    settle(dve)
                    for k in range(size * CB):
                        last = nc.vector.bn_aggr(MV[:, k, :], ST[:, k, :])
                    chain.link(last)
                    nc.vector.tensor_copy(MVS[:, bass.ds(u * (2 * CB), size * CB), :], MV[:, 0:size * CB, :]).then_inc(s_var, 1)

                def scales(u, size):
                    done = u + (n * UNITS + 1)
                    dve.wait_ge(s_sd, done)
                    nc.vector.reciprocal(blocks(RS, u, size), blocks(SD, u, size)).then_inc(s_rs, 1)
                    dve.wait_ge(s_rs, done)
                    nc.vector.scalar_tensor_tensor(blocks(NM, u, size), MVS[:, bass.ds(u * (2 * CB), size * CB), 0], -1.0,
                                                   blocks(RS, u, size), ALU.mult, ALU.mult).then_inc(s_ln, 1)
                statistics(0, 2)
                with dve.Fori(1, UNITS - 1) as u:
                    statistics(u, 2)
                    scales(u - 1, 2)
                statistics(UNITS - 1, 1)
                scales(UNITS - 2, 2)
                scales(UNITS - 1, 1)
                chain.done(UNITS, 2)

            dve.wait_ge(s_x, 32)
            norm(0)

            def start0(c, par):
                dve.wait_ge(s_tp, c + 1)
                nc.vector.tensor_scalar(wide(ACC, c), PS[:, par, :], cols[:, E1:E1 + 1], None, ALU.mult).then_inc(s_acc0, 1)
            chunks(dve, start0)

            iota_b = iota_row[:].unsqueeze(1).to_broadcast([P, GT, P])

            def onehot(i, q, slot):
                where = LD[:, bass.ds(i * (RING * GT) + q * GT, GT)].unsqueeze(2).to_broadcast([P, GT, P])
                nc.vector.tensor_tensor(OH[:, slot * GT:(slot + 1) * GT, :], iota_b, where, ALU.is_equal).then_inc(s_oh, 1)

            def add(i, q, a, starts, grouped, degrees=False):
                b = q % 2
                first = i * (RING * GT) + q * GT
                dve.wait_ge(s_mm, mm(i * RING + (q + a * GROUPS)))
                if grouped:
                    dve.wait_ge(s_add, first + (a * T + GT * CREDIT))
                    if degrees:
                        w = AD[:, :, bass.ds(starts[q], P)]
                        nc.vector.tensor_tensor(w, w, PS[:, 2 * b:2 * b + 2, 0:P], ALU.add).then_inc(s_add, GT)
                    else:
                        w = ACC[:, bass.ds(starts[q], P)]
                        nc.vector.tensor_tensor(w, w, PS[:, 2 * b, 0:P], ALU.add).then_inc(s_add, GT)
                    return
                for k in range(GT):
                    dve.wait_ge(s_add, first + (a * T + GT * CREDIT + k))
                    if degrees:
                        w = AD[:, :, bass.ds(starts[q * GT + k], P)]
                        nc.vector.tensor_tensor(w, w, PS[:, 2 * b:2 * b + 2, k * P:(k + 1) * P], ALU.add).then_inc(s_add, 1)
                    else:
                        w = ACC[:, bass.ds(starts[q * GT + k], P)]
                        nc.vector.tensor_tensor(w, w, PS[:, 2 * b, k * P:(k + 1) * P], ALU.add).then_inc(s_add, 1)

            def turns(produce, consume, lead=1, windows=True):
                def all_turns(grouped):
                    starts = lambda i: window_starts(mybir.EngineType.DVE, i, grouped) if windows else None
                    for q in range(lead):
                        produce(0, q)
                    with dve.Fori(0, ITERS - 1) as i:
                        here = starts(i)
                        for q in range(RING):
                            produce(*((i, q + lead) if q + lead < RING else (i + 1, q + lead - RING)))
                            consume(i, q, here, grouped)
                    here = starts(ITERS - 1)
                    for q in range(RING):
                        if q + lead < RING:
                            produce(ITERS - 1, q + lead)
                        consume(ITERS - 1, q, here, grouped)
                if windows:
                    either(dve, all_turns)
                else:
                    all_turns(False)

            def multiplied(i, q, a, back):
                dve.wait_ge(s_mm, mm(i * RING + (q - back + a * GROUPS)))

            def add_bias(n):
                dve.wait_ge(s_h, (2 * n + 1) * CHUNKS)
                nc.vector.tensor_tensor(X[:], X[:], rows[:, n:n + 1, :].to_broadcast([P, NBP, P]), ALU.add)
            add_bias(0)

            def message0(i, q):
                b = q % 2
                multiplied(i, q, A0, 2)
                dve.wait_ge(s_gath[q], i * (16 * GT) + 16 * GT)
                extra = 16 if q == (tail_slot // GT) and isinstance(i, int) and i == ITERS - 1 else 0
                dve.wait_ge(s_ea[q], i * 16 + (16 + extra))
                nc.vector.tensor_tensor(MSG[:, b * GT:(b + 1) * GT, :], G[:, q * GT:(q + 1) * GT, :],
                                        EA[:, q * GT:(q + 1) * GT, :], ALU.add).then_inc(s_msg, 1)
                onehot(i, q, q)
            turns(message0, lambda i, q, starts, grouped: add(i, q, A0, starts, grouped))

            norm(1, 0)

            dve.wait_ge(s_h, 2 * CHUNKS)
            nc.vector.tensor_tensor(X[:], X[:], H[:], ALU.add)
            dve.wait_ge(s_deg0, 1)
            def produce1(i, q):
                multiplied(i, q, A1, RING)
                onehot(i, q, q)
            turns(produce1, lambda i, q, starts, grouped: add(i, q, A1, starts, grouped, degrees=True), 2)

            for c in range(CHUNKS):
                n0 = c * CB * P
                w = min(CB * P, N - n0)
                dve.wait_ge(s_y, c + 1)
                last = nc.vector.bn_stats(ST[:, c, :], ACC[:, n0:n0 + w])
            chain.one(last)
            chain.one(nc.vector.bn_aggr(small[:, 0:2], ST[:, 0:CHUNKS, :].rearrange("p c s -> p (c s)")))
            nc.vector.tensor_scalar(small[:, 4:5], small[:, 1:2], BN_EPS, None, ALU.add).then_inc(s_bva, 1)
            dve.wait_ge(s_bsd, 1)
            chain.one(nc.vector.reciprocal(small[:, 4:5], small[:, 4:5]))
            chain.one(nc.vector.tensor_tensor(small[:, 2:3], small[:, 4:5], cols[:, GAM:GAM + 1], ALU.mult))
            chain.one(nc.vector.tensor_tensor(small[:, 5:6], small[:, 0:1], small[:, 2:3], ALU.mult))
            nc.vector.tensor_tensor(small[:, 3:4], cols[:, BET:BET + 1], small[:, 5:6], ALU.subtract).then_inc(s_bns, 1)
            norm(2, 1)
            dve.wait_ge(s_seg, 16 * 2 * HEADS)
            new_i, keep_i = NEW.bitcast(i32), KEEP.bitcast(i32)
            chain.one(nc.vector.tensor_tensor(NEW, new_i, keep_i, ALU.not_equal))
            chain.one(nc.vector.tensor_scalar(KEEP, NEW, -1.0, 1.0, ALU.mult, ALU.add))
            chain.one(nc.vector.tensor_scalar(NEW, NEW, -BIG, None, ALU.mult))

            add_bias(1)
            ROOTS = -(-NW // ITERS)
            assert ROOTS * (ITERS - 1) < NW
            def produce_a(i, q):
                dve.wait_ge(s_ohtp, i * RING + (q + 1 - 2)) if (isinstance(i, int) and i * RING + q >= 2) or not isinstance(i, int) else None
                onehot(i, q, q % 2)

            def leaky(i, q, *_):
                b = q % 2
                dve.wait_ge(s_sl, i * RING + (q + 1))
                m = MSG[:, b * GT:(b + 1) * GT, :].rearrange("p k f -> p (k f)")
                nc.vector.tensor_tensor(m, m, PS[:, 2 + b, :], ALU.max).then_inc(s_lk, 1)
                if q == 0:
                    n = NW - ROOTS * (ITERS - 1) if isinstance(i, int) and i == ITERS - 1 else ROOTS
                    some = DEG[:, bass.ds(i * ROOTS, n)]
                    nc.vector.reciprocal(some, some)
            dve.wait_ge(s_dsd, 1)
            turns(produce_a, leaky, 2, windows=False)

            el_view = EL[:].rearrange("p (j g) h -> p g h j", g=SEG)
            dve.wait_ge(s_el, GROUPS + CREDIT)
            nc.vector.tensor_copy(F.rearrange("p (g h j) -> p g h j", g=SEG, h=HEADS), el_view).then_inc(s_sort, 1)
            dve.wait_ge(s_scc, -(-SEG // GT))
            resolved = [0]
            local = H[:, 0:SEG, :].rearrange("p b f -> p (b f)")

            def scan(gate, data, join, outward, backward, initial):
                turn = (lambda ap: ap[:, ::-1]) if backward else (lambda ap: ap)
                chain.one(nc.vector.tensor_tensor_scan(turn(local), turn(gate), turn(data), initial, outward, join))
                end = local[:, 0:1] if backward else local[:, SL - 1:SL]
                nc.vector.tensor_copy(small[:, 0:1], end)
                nc.vector.tensor_reduce(small[:, 1:2], gate, AX.X, ALU.min).then_inc(s_cr, 1)
                resolved[0] += 1
                dve.wait_ge(s_crt, resolved[0])
                nc.vector.memset(carry[:], initial)
                chain.one(nc.vector.tensor_copy(carry_rows[:], PS[0:1, 6, 0:2 * P]))
                for h in range(HEADS):
                    data_h = carry_rows[0:1, h * CHAINS:(h + 1) * CHAINS]
                    gate_h = carry_rows[0:1, P + h * CHAINS:P + (h + 1) * CHAINS]
                    to = carry[0:1, h, 0:CHAINS] if backward else carry[0:1, h, 1:CHAINS + 1]
                    last = nc.vector.tensor_tensor_scan(turn(to), turn(gate_h), turn(data_h), initial, outward, join)
                chain.one(last)
                nc.vector.tensor_copy(carry_rows[:, 0:P].rearrange("p (h j) -> p h j", h=HEADS),
                                      carry[:, :, 1:CHAINS + 1] if backward else carry[:, :, 0:CHAINS]).then_inc(s_ci, 1)
                dve.wait_ge(s_cit, resolved[0])
                chain.one(nc.vector.tensor_copy(small[:, 2:3], PS[:, 7, 0:1]))
                return turn, gate, data, small[:, 2:3], outward, join

            def finish(to, turn, gate, data, first, outward, join):
                chain.one(nc.vector.tensor_tensor_scan(turn(to), turn(gate), turn(data), first, outward, join))

            ahead, behind = NEW[:, 1:SL + 1], NEW[:, 0:SL]
            finish(F, *scan(behind, S, ALU.max, ALU.add, False, -BIG))
            finish(F, *scan(ahead, F, ALU.max, ALU.add, True, -BIG))
            nc.vector.tensor_tensor(S, S, F, ALU.subtract).then_inc(s_sub, 1)
            dve.wait_ge(s_exp, 1)
            finish(F, *scan(KEEP[:, 0:SL], S, ALU.add, ALU.mult, False, 0.0))
            finish(F, *scan(ahead, F, ALU.max, ALU.add, True, -BIG))
            chain.one(nc.vector.tensor_scalar(F, F, 1e-16, None, ALU.max))
            chain.one(nc.vector.reciprocal(F, F))
            nc.vector.tensor_tensor(S, S, F, ALU.mult).then_inc(s_al, 1)
            for n, g in enumerate(range(0, SEG, GT)):
                w = min(GT, SEG - g)
                dve.wait_ge(s_alt, n + 1)
                last = nc.vector.tensor_copy(el_view[:, g:g + w], PS[:, n % 2, 0:w * P].rearrange("p (g h j) -> p g h j", g=w, h=HEADS))
                last.then_inc(s_alc, 1)
            dve.wait_ge(s_az, 1)

            def message_b(i, q):
                multiplied(i, q, AB, RING)
                onehot(i, q, q)
            turns(message_b, lambda i, q, starts, grouped: add(i, q, AB, starts, grouped), 2)
            norm(3, 2)

            def scale3(c, par):
                dve.wait_ge(s_tp, c + (3 * CHUNKS + 1))
                nc.vector.tensor_tensor(wide(HT, c), PS[:, par, :], wide(DEG, c), ALU.mult).then_inc(s_acc0, 1)
            chunks(dve, scale3)

            def produce3(i, q):
                multiplied(i, q, A3, RING)
                onehot(i, q, q)
            dve.wait_ge(s_ht, 2 * CHUNKS)
            turns(produce3, lambda i, q, starts, grouped: add(i, q, A3, starts, grouped), 2)
            dve.wait_ge(s_add, added(4 * GROUPS - 1))

            def times_dinv(c, par):
                nc.vector.tensor_tensor(MSG[:, par * GT:(par + 1) * GT, :].rearrange("p k f -> p (k f)"),
                                        wide(ACC, c), wide(DEG, c), ALU.mult).then_inc(s_dv, 1)
            links = 1

            def last_rows(c, par):
                chain.at(c, links)
                dve.wait_ge(s_m2, c + (3 * CHUNKS + 1))
                h, xr = (nodes(v, c).rearrange("p b f -> p (b f)") for v in (H, X))
                chain.link(nc.vector.tensor_tensor(h, h, PS[:, 6 + par, :], ALU.add))
                nc.vector.scalar_tensor_tensor(xr, h, 0.0, xr, ALU.max, ALU.add).then_inc(s_x1, 1)
            times_dinv(0, 0)
            with dve.Fori(0, CHUNKS // 2) as j:
                for par in range(2):
                    times_dinv(2 * j + (par + 1), 1 - par)
                    last_rows(2 * j + par, par)
            last_rows(CHUNKS - 1, 0)
            chain.done(CHUNKS, links)
            with dve.If(disordered(dve) != 0):
                with dve.Fori(0, NB) as b:
                    dve.wait_ge(s_ug, b * 16 + DMA_CREDIT)
                    nc.vector.tensor_copy(IDX[:, 0:1], LABEL[:, bass.ds(b, 1)]).then_inc(s_ui, 1)

        @block.tensor
        def _(pe):
            pe.sem_inc(s_mm, CREDIT)
            pe.wait_ge(s_pre, 3)
            pe.wait_ge(s_f, 1)
            def transpose_edges():
                for g in range(TG):
                    bank, off = divmod(g * P, GT * P)
                    nc.tensor.transpose(PS[:, bank, off:off + P], src_f[:, g, :], ident[:])
                    nc.tensor.transpose(PS[:, 2 + bank, off:off + P], loc_f[:, g, :], ident[:])
                    last = nc.tensor.transpose(PS[0:1, 4 + bank, off:off + P], dst_f[:, g, 0:1], ident[:])
                return last
            transpose_edges().then_inc(s_tp0, 1)
            pe.wait_ge(s_bad, 1)
            nc.tensor.transpose(PS[0:1, 7, 0:P], small[:, 6:7], ident[:]).then_inc(s_badt, 1)
            pe.wait_ge(s_flag, 1)
            with pe.If(disordered(pe) != 0):
                for g in range(TG):
                    bank, off = divmod(g * P, GT * P)
                    last = nc.tensor.transpose(PS[:, 4 + bank, off:off + P], dst_f[:, g, :], ident[:])
                last.then_inc(s_sdst, 1)
                pe.wait_ge(s_shits, 1)
                for c in range(CHUNKS):
                    if c >= 2:
                        pe.wait_ge(s_scc2, c - 1)
                    nc.tensor.matmul(PS[:, c % 2, :], ones[:], PLACE[:, c * CB * P:(c + 1) * CB * P], start=True, stop=True).then_inc(s_scnt, 1)
                pe.wait_ge(s_scc2, CHUNKS)
                with pe.Fori(0, T) as t:
                    pe.wait_ge(s_soh, t + 1)
                    for c in range(CHUNKS):
                        chunk = HITS[:, c * CB * P:(c + 1) * CB * P]
                        pe.wait_ge(s_sq, t * CHUNKS + (c + 1))
                        nc.tensor.matmul(PS[:, 2 * (c % 2), :], lower, chunk, start=True, stop=True)
                        nc.tensor.matmul(PS[:, 2 * (c % 2) + 1, :], ones[:], chunk, start=True, stop=True).then_inc(s_sp, 1)
                pe.wait_ge(s_sf, 1)
                transpose_edges().then_inc(s_stp, 1)

            def spread_distances(grouped):
                if grouped:
                    for bank, n0 in enumerate(range(0, T, GT * P)):
                        last = nc.tensor.matmul(PS[:, 4 + bank, 0:min(GT * P, T - n0)], ones[0:1, :], away[:, n0:min(T, n0 + GT * P)], start=True, stop=True)
                    last.then_inc(s_awp, 1)
                else:
                    pe.wait_ge(s_awd, 1)
            either(pe, spread_distances)
            pe.wait_ge(s_w, 16 * 18)
            nc.tensor.transpose(PS[:, 6, 0:P], W["ln_raw"][:], ident[:]).then_inc(s_tp0, 1)
            pe.wait_ge(s_ix, 2)

            def block_of(buf, c, k):
                at = (c * CB + k) * P
                return buf[:, at:at + P]

            def transpose_h(n, taken, per):
                for c in range(CHUNKS):
                    pe.wait_ge(s_h, n * CHUNKS + c + 1)
                    if c >= 2:
                        for s, before in taken:
                            pe.wait_ge(s, before + c - 1)
                    for k in range(CB):
                        last = nc.tensor.transpose(PS[:, c % 2, k * P:(k + 1) * P], H[:, c * CB + k, :], ident[:])
                    last.then_inc(s_tp, 1)

            def aggregate(a, ready, degrees=False, rows_of=lambda q: (MSG, (q % 2) * GT)):
                def all_turns(grouped):
                    with pe.Fori(0, ITERS) as i:
                        for q in range(RING):
                            b = q % 2
                            pe.wait_ge(s_add, added(i * RING + (q - 2 + a * GROUPS)))
                            ready(i, q)
                            buf, at = rows_of(q)
                            for k in range(GT):
                                to = slice(0, P) if grouped else slice(k * P, (k + 1) * P)
                                first, final = not grouped or k == 0, not grouped or k == GT - 1
                                last = nc.tensor.matmul(PS[:, 2 * b, to], buf[:, at + k, :], OH[:, q * GT + k, :], start=first, stop=final)
                                if degrees:
                                    last = nc.tensor.matmul(PS[:, 2 * b + 1, to], ones[:], OH[:, q * GT + k, :], start=first, stop=final)
                            last.then_inc(s_mm, 1)
                either(pe, all_turns)

            def ohs(n, i, q):
                pe.wait_ge(s_oh, i * RING + (n * GROUPS + q + 1))

            transpose_h(0, [(s_acc0, 0)], 1)
            pe.wait_ge(s_acc0, CHUNKS)

            def ready0(i, q):
                ohs(0, i, q)
                pe.wait_ge(s_relu, i * RING + (q + 1))
            aggregate(A0, ready0)

            def perceptron_in(n, w):
                def one(c):
                    if c >= 2:
                        pe.wait_ge(s_z, n * CHUNKS + c - 1)
                    nc.tensor.matmul(PS[:, 4 + c % 2, :], W[w][:], ACC[:, c * CB * P:(c + 1) * CB * P], start=True, stop=True).then_inc(s_m1, 1)
                return one

            pe.wait_ge(s_add, added(GROUPS - 1))
            first = perceptron_in(0, "g0_1")
            first(0)
            for c in range(CHUNKS):
                if c + 1 < CHUNKS:
                    first(c + 1)
                pe.wait_ge(s_z, c + 1)
                if c >= 2:
                    pe.wait_ge(s_rows, c - 1)
                for k in range(CB):
                    last = nc.tensor.matmul(PS[:, 6 + c % 2, k * P:(k + 1) * P], MSG[:, (c % 2) * GT + k, :], W["g0_2"][:], start=True, stop=True)
                last.then_inc(s_m2, 1)

            transpose_h(1, [(s_acc0, CHUNKS)], 1)
            pe.wait_ge(s_acc0, 2 * CHUNKS)

            def ready1(i, q):
                ohs(1, i, q)
                pe.wait_ge(s_gath[q], i * (16 * GT) + 16 * GT * (G1 * ITERS + 1))
            aggregate(A1, ready1, True, lambda q: (G, q * GT))

            pe.wait_ge(s_add, added(2 * GROUPS - 1))
            first = perceptron_in(1, "g1_1")
            first(0)
            for c in range(CHUNKS):
                if c + 1 < CHUNKS:
                    first(c + 1)
                pe.wait_ge(s_z, CHUNKS + c + 1)
                if c >= 2:
                    pe.wait_ge(s_y, c - 1)
                nc.tensor.matmul(PS[:, 6 + c % 2, :], W["g1_2"][:], MSG[:, (c % 2) * GT:(c % 2 + 1) * GT, :].rearrange("p k f -> p (k f)"),
                                 start=True, stop=True).then_inc(s_yp, 1)
            for c in range(CHUNKS):
                pe.wait_ge(s_bn, c + 1)
                if c >= 2:
                    pe.wait_ge(s_rows, CHUNKS + c - 1)
                for k in range(CB):
                    to = PS[:, 4 + c % 2, k * P:(k + 1) * P]
                    last = nc.tensor.matmul(to, block_of(ACC, c, k), ident[:], start=True, stop=True)
                last.then_inc(s_m2, 1)

            transpose_h(2, [(s_ht, 0)], 1)
            for c in range(CHUNKS):
                pe.wait_ge(s_ht, c + 1)
                if c >= 2:
                    pe.wait_ge(s_lrc, c - 1)
                for k in range(CB):
                    last = nc.tensor.matmul(PS[:, 4 + 2 * (c % 2) + k // 2, (k % 2) * 2 * P:(k % 2 + 1) * 2 * P],
                                            block_of(HT, c, k), WLR[:], start=True, stop=True)
                last.then_inc(s_lrp, 1)

            pe.wait_ge(s_lrc, CHUNKS)

            def flip(i, q):
                b = q % 2
                ohs(2, i, q)
                if not (isinstance(i, int) and i * RING + q < 2):
                    pe.wait_ge(s_oht, i * RING + (q + 1 - 2))
                for k in range(GT):
                    last = nc.tensor.transpose(PS[:, b, k * P:(k + 1) * P], OH[:, b * GT + k, :], ident[:])
                last.then_inc(s_ohtp, 1)

            def sums(i, q, grouped):
                b = q % 2
                pe.wait_ge(s_oht, i * RING + (q + 1))
                each = 16 if grouped else 16 * GT
                pe.wait_ge(s_win[q], i * each + each)
                pe.wait_ge(s_gath[q], i * (16 * GT) + 16 * GT * (GA * ITERS + 1))
                if not (isinstance(i, int) and i * RING + q < 2):
                    pe.wait_ge(s_lk, i * RING + (q + 1 - 2))
                if grouped:
                    nc.tensor.matmul(PS[:, 2 + b, :], EA[:, q * GT, :], OHT[:, b * GT:(b + 1) * GT, :].rearrange("p k f -> p (k f)"),
                                     start=True, stop=False)
                for k in range(GT):
                    to = PS[:, 2 + b, k * P:(k + 1) * P]
                    if not grouped:
                        nc.tensor.matmul(to, EA[:, q * GT + k, :], OHT[:, b * GT + k, :], start=True, stop=False)
                    last = nc.tensor.matmul(to, G[:, q * GT + k, :], ident[:], start=False, stop=not grouped or k == GT - 1)
                last.then_inc(s_zz, 1)

            def logits(i, q):
                b = q % 2
                pe.wait_ge(s_lk, i * RING + (q + 1))
                pe.wait_ge(s_el, i * RING + (q + 1 + CREDIT - 2))
                for k in range(GT):
                    last = nc.tensor.matmul(PS[:, 4 + b, k * HEADS:(k + 1) * HEADS], MSG[:, b * GT + k, :], att4[:], start=True, stop=True)
                last.then_inc(s_lg, 1)

            def attend(i, q, grouped):
                if q < RING - 1:
                    flip(i, q + 1)
                elif not isinstance(i, int) or i < ITERS - 1:
                    flip(i + 1, 0)
                sums(i, q, grouped)
                if q > 0:
                    logits(i, q - 1)
                elif not isinstance(i, int) or i > 0:
                    logits(i - 1, RING - 1)
            def attention(grouped):
                flip(0, 0)
                for q in range(RING):
                    attend(0, q, grouped)
                with pe.Fori(1, ITERS - 1) as i:
                    for q in range(RING):
                        attend(i, q, grouped)
                for q in range(RING):
                    attend(ITERS - 1, q, grouped)
                logits(ITERS - 1, RING - 1)
            either(pe, attention)

            pe.wait_ge(s_sort, 1)
            for n, g in enumerate(range(0, SEG, GT)):
                if n >= 2:
                    pe.wait_ge(s_scc, n - 1)
                for k in range(min(GT, SEG - g)):
                    last = nc.tensor.transpose(PS[:, n % 2, k * P:(k + 1) * P], F[:, (g + k) * P:(g + k + 1) * P], ident[:])
                last.then_inc(s_sc, 1)

            for n in range(4):
                pe.wait_ge(s_cr, n + 1)
                nc.tensor.transpose(PS[0:1, 6, 0:P], small[:, 0:1], ident[:])
                nc.tensor.transpose(PS[0:1, 6, P:2 * P], small[:, 1:2], ident[:]).then_inc(s_crt, 1)
                pe.wait_ge(s_ci, n + 1)
                nc.tensor.transpose(PS[:, 7, 0:1], carry_rows[:, 0:P], ident[0:1, 0:1]).then_inc(s_cit, 1)

            pe.wait_ge(s_al, 1)
            for n, g in enumerate(range(0, SEG, GT)):
                if n >= 2:
                    pe.wait_ge(s_alc, n - 1)
                for k in range(min(GT, SEG - g)):
                    last = nc.tensor.transpose(PS[:, n % 2, k * P:(k + 1) * P], S[:, (g + k) * P:(g + k + 1) * P], ident[:])
                last.then_inc(s_alt, 1)

            pe.wait_ge(s_alc, -(-SEG // GT))

            def ready_b(i, q):
                ohs(3, i, q)
                pe.wait_ge(s_msg, i * RING + (GROUPS + CREDIT + q + 1))
            aggregate(AB, ready_b, False, lambda q: (G, q * GT))

            pe.wait_ge(s_add, added(3 * GROUPS - 1))
            for c in range(CHUNKS):
                if c >= 2:
                    pe.wait_ge(s_rows, 2 * CHUNKS + c - 1)
                for k in range(CB):
                    to = PS[:, 6 + c % 2, k * P:(k + 1) * P]
                    last = nc.tensor.matmul(to, block_of(ACC, c, k), ident[:], start=True, stop=True)
                last.then_inc(s_m2, 1)

            transpose_h(3, [(s_acc0, 2 * CHUNKS)], 1)
            for c in range(CHUNKS):
                pe.wait_ge(s_acc0, 2 * CHUNKS + c + 1)
                if c >= 2:
                    pe.wait_ge(s_lrc, CHUNKS + c - 1)
                    pe.wait_ge(s_ht, CHUNKS + c - 1)
                for k in range(CB):
                    nc.tensor.matmul(PS[:, 4 + c % 2, k * P:(k + 1) * P], block_of(HT, c, k), W["g3"][:], start=True, stop=True)
                nc.tensor.matmul(PS[:, 6 + c % 2, :], W["g3"][:], HT[:, c * CB * P:(c + 1) * CB * P], start=True, stop=True).then_inc(s_lrp, 1)

            def ready3(i, q):
                ohs(4, i, q)
                pe.wait_ge(s_gath[q], i * (16 * GT) + 16 * GT * (G3 * ITERS + 1))
            aggregate(A3, ready3, False, lambda q: (G, q * GT))
            for c in range(CHUNKS):
                pe.wait_ge(s_z, 2 * CHUNKS + c + 1)
                if c >= 2:
                    pe.wait_ge(s_x1, c - 1)
                for k in range(CB):
                    last = nc.tensor.matmul(PS[:, 6 + c % 2, k * P:(k + 1) * P], MSG[:, (c % 2) * GT + k, :], W["ln"][:], start=True, stop=True)
                last.then_inc(s_m2, 1)


_INS = ["x", "src", "dst", "edge_attr_128", "L0_gnn_W1", "L0_gnn_b1", "L0_gnn_W2", "L0_gnn_b2", "L0_gnn_eps",
        "L1_gnn_W1", "L1_gnn_b1", "L1_gnn_W2", "L1_gnn_b2", "L1_gnn_gamma", "L1_gnn_beta", "L2_gnn_weight_l",
        "L2_gnn_weight_r", "L2_gnn_att", "L2_gnn_bias", "L3_gnn_W_gcn", "L3_gnn_b_gcn", "L3_gnn_W_ln"]


def kernel(**inputs):
    import numpy as _np
    import concourse.bacc as _bacc
    from concourse import mybir as _mybir
    from concourse.bass_utils import run_bass_kernel_spmd as _run

    nc = _bacc.Bacc("TRN2", target_bir_lowering=False, num_devices=1)
    arrays, args = {}, []
    for name in _INS:
        a = _np.ascontiguousarray(inputs[name])
        arrays[f"in_{name}_dram"] = a
        args.append(nc.dram_tensor(f"in_{name}_dram", a.shape, _mybir.dt.from_np(a.dtype), kind="ExternalInput").ap())
    shape = _np.shape(inputs["x"])
    args.append(nc.dram_tensor("out_0_dram", shape, _mybir.dt.float32, kind="ExternalOutput").ap())
    build(nc, *args)
    r = _run(nc, [arrays], core_ids=[0])
    return r.results[0]["out_0_dram"]
```
